# Optimizing a Trainium2 kernel written in Bass

```python
import numpy as np
import jax
import jax.numpy as jnp

def _softmax(x, axis=-1):
    return jax.nn.softmax(x, axis=axis)

def _gelu(x):
    return jax.nn.gelu(x, approximate=True)

def _silu(x):
    return jax.nn.silu(x)

def _sigmoid(x):
    return jax.nn.sigmoid(x)

def _layernorm(x, axis=-1, eps=1e-05):
    m = jnp.mean(x, axis=axis, keepdims=True)
    v = jnp.var(x, axis=axis, keepdims=True)
    return (x - m) / jnp.sqrt(v + eps)

def _scatter_add(tgt, idx, src, axis=0):
    return tgt.at[idx].add(src)

def _segment_sum(src, seg, n):
    return jax.ops.segment_sum(src, seg, n)
kernel_name = 'mk_xattn_ffn_d1_seqx_r2_04179d'

def setup_inputs(seed: int=0):
    np.random.seed(seed)
    _w = jnp.asarray

    def _rec_inputs():
        import jax
        import jax.numpy as jnp
        _rk = jax.random.key(seed)
        x = -0.0003929 + 0.9999 * jax.random.normal(jax.random.fold_in(_rk, 1), (16, 256, 2048), jnp.float32)
        _lenS = 256 - jax.random.randint(jax.random.fold_in(_rk, 7), (16,), 0, max(1, 256 // 4) + 1, jnp.int32)
        _lenS2 = 256 - jax.random.randint(jax.random.fold_in(_rk, 8), (16,), 0, max(1, 256 // 4) + 1, jnp.int32)
        _ctx_4096P = jax.random.normal(jax.random.fold_in(_rk, 11), (16, 16, 2048), jnp.float32)
        _ctx_4096c = jax.random.dirichlet(jax.random.fold_in(_rk, 511), 0.3 * jnp.ones((16,), jnp.float32), (16, 256))
        _ctx_4096t = jnp.einsum('bsk,bkd->bsd', _ctx_4096c, _ctx_4096P)
        _ctx_4096t = _ctx_4096t * jax.lax.rsqrt(jnp.mean(jnp.square(_ctx_4096t)) + 1e-12) * 0.953939
        ctx_4096 = 2.81802e-05 + 1.00001 * (_ctx_4096t + 0.3 * jax.random.normal(jax.random.fold_in(_rk, 611), (16, 256, 2048), jnp.float32))
        return (x, ctx_4096)
    x, ctx_4096 = _rec_inputs()

    def _L0_xattn_setup():
        import jax, jax.numpy as jnp
        import numpy as np
        DIM = 256
        HEADS = 8
        DIM_HEAD = 64
        HIDDEN = HEADS * DIM_HEAD
        SCALE = DIM_HEAD ** (-0.5)
        key = jax.random.key(seed)
        ks = jax.random.split(key, 9)
        b, n = (8, 2048)
        std = 1.0 / np.sqrt(DIM)
        return {'q': jax.random.normal(ks[0], (b, DIM, n), jnp.float32), 'k': jax.random.normal(ks[1], (b, DIM, n), jnp.float32), 'v': jax.random.normal(ks[2], (b, DIM, n), jnp.float32), 'Wq': jax.random.normal(ks[3], (HIDDEN, DIM), jnp.float32) * std, 'Wk': jax.random.normal(ks[4], (HIDDEN, DIM), jnp.float32) * std, 'Wv': jax.random.normal(ks[5], (HIDDEN, DIM), jnp.float32) * std, 'Wo': jax.random.normal(ks[6], (DIM, HIDDEN), jnp.float32) * (1.0 / np.sqrt(HIDDEN)), 'bo': jax.random.normal(ks[7], (DIM,), jnp.float32) * 0.01, 'g': jnp.ones((1, DIM, 1), jnp.float32)}
    _L0_xattn_all = _L0_xattn_setup()
    _L0_xattn_in = {k: v for k, v in _L0_xattn_all.items() if k in ('Wq', 'Wk', 'Wv', 'Wo', 'bo', 'g')}
    del _L0_xattn_all

    def _L0_ffn_setup():
        import jax, jax.numpy as jnp
        import numpy as np
        N_STREAMS = 4
        DIM = 512
        SINKHORN_ITERS = 50
        SINKHORN_TAU = 0.1
        RMS_EPS = 1.1920929e-07

        def sinkhorn_log(logits, num_iters=SINKHORN_ITERS, tau=SINKHORN_TAU):
            Z = logits / tau
            u0 = jnp.zeros(Z.shape[:-1], Z.dtype)
            v0 = jnp.zeros_like(u0)

            def step(carry, _):
                u, v = carry
                u = -jax.nn.logsumexp(Z + v[..., None, :], axis=-1)
                v = -jax.nn.logsumexp(Z + u[..., :, None], axis=-2)
                return ((u, v), None)
            (u, v), _ = jax.lax.scan(step, (u0, v0), None, length=num_iters)
            return jnp.exp(Z + u[..., :, None] + v[..., None, :])
        key = jax.random.key(seed)
        ks = jax.random.split(key, 6)
        B, T = (4, 1024)
        n, C = (N_STREAMS, DIM)
        wd = n * C
        x = jax.random.normal(ks[0], (B, T, wd), dtype=jnp.float32)
        W_res = 0.01 * jax.random.normal(ks[1], (n * n, wd), dtype=jnp.float32)
        W_pre = 0.01 * jax.random.normal(ks[2], (n, wd), dtype=jnp.float32)
        W_post = 0.01 * jax.random.normal(ks[3], (n, wd), dtype=jnp.float32)
        H_res_base = jnp.full((n, n), -0.5, dtype=jnp.float32)
        H_res_base = H_res_base.at[jnp.arange(n), jnp.arange(n)].set(0.0)
        H_pre_base = jnp.zeros((n,), dtype=jnp.float32).at[0].set(1.0)
        H_post_base = jnp.zeros((n,), dtype=jnp.float32)
        gate = jnp.array([5.0], dtype=jnp.float32)
        W_branch = 1.0 / np.sqrt(C) * jax.random.normal(ks[4], (C, C), dtype=jnp.float32)
        return {'x': x, 'W_res': W_res, 'W_pre': W_pre, 'W_post': W_post, 'H_res_base': H_res_base, 'H_pre_base': H_pre_base, 'H_post_base': H_post_base, 'gate': gate, 'W_branch': W_branch}
    _L0_ffn_all = _L0_ffn_setup()
    _L0_ffn_in = {k: v for k, v in _L0_ffn_all.items() if k in ('W_res', 'W_pre', 'W_post', 'H_res_base', 'H_pre_base', 'H_post_base', 'gate', 'W_branch')}
    del _L0_ffn_all
    return {'x': x, 'ctx_4096': ctx_4096, 'L0_xattn_Wq': _L0_xattn_in['Wq'], 'L0_xattn_Wk': _L0_xattn_in['Wk'], 'L0_xattn_Wv': _L0_xattn_in['Wv'], 'L0_xattn_Wo': _L0_xattn_in['Wo'], 'L0_xattn_bo': _L0_xattn_in['bo'], 'L0_xattn_g': _L0_xattn_in['g'], 'L0_ffn_W_res': _L0_ffn_in['W_res'], 'L0_ffn_W_pre': _L0_ffn_in['W_pre'], 'L0_ffn_W_post': _L0_ffn_in['W_post'], 'L0_ffn_H_res_base': _L0_ffn_in['H_res_base'], 'L0_ffn_H_pre_base': _L0_ffn_in['H_pre_base'], 'L0_ffn_H_post_base': _L0_ffn_in['H_post_base'], 'L0_ffn_gate': _L0_ffn_in['gate'], 'L0_ffn_W_branch': _L0_ffn_in['W_branch']}

def reference(x, ctx_4096, L0_xattn_Wq, L0_xattn_Wk, L0_xattn_Wv, L0_xattn_Wo, L0_xattn_bo, L0_xattn_g, L0_ffn_W_res, L0_ffn_W_pre, L0_ffn_W_post, L0_ffn_H_res_base, L0_ffn_H_pre_base, L0_ffn_H_post_base, L0_ffn_gate, L0_ffn_W_branch):
    import jax
    import jax.numpy as jnp

    def _L0_xattn_ref(q, k, v, Wq, Wk, Wv, Wo, bo, g):
        import jax, jax.numpy as jnp
        import numpy as np
        DIM = 256
        HEADS = 8
        DIM_HEAD = 64
        HIDDEN = HEADS * DIM_HEAD
        SCALE = DIM_HEAD ** (-0.5)
        b = q.shape[0]
        qh = jnp.einsum('bcn,oc->bon', q, Wq).reshape(b, HEADS, DIM_HEAD, -1)
        kh = jnp.einsum('bcn,oc->bon', k, Wk).reshape(b, HEADS, DIM_HEAD, -1)
        vh = jnp.einsum('bcn,oc->bon', v, Wv).reshape(b, HEADS, DIM_HEAD, -1)
        qh = jax.nn.softmax(qh, axis=-2) * SCALE
        kh = jax.nn.softmax(kh, axis=-1)
        context = jnp.einsum('bhdn,bhen->bhde', kh, vh)
        out = jnp.einsum('bhde,bhdn->bhen', context, qh)
        out = out.reshape(b, HIDDEN, -1)
        out = jnp.einsum('bcn,oc->bon', out, Wo) + bo[None, :, None]
        norm = jnp.maximum(jnp.sqrt(jnp.sum(out * out, axis=1, keepdims=True)), 1e-12)
        return out / norm * g * np.sqrt(DIM)

    def _L0_ffn_ref(x, W_res, W_pre, W_post, H_res_base, H_pre_base, H_post_base, gate, W_branch):
        import jax, jax.numpy as jnp
        import numpy as np
        N_STREAMS = 4
        DIM = 512
        SINKHORN_ITERS = 50
        SINKHORN_TAU = 0.1
        RMS_EPS = 1.1920929e-07

        def sinkhorn_log(logits, num_iters=SINKHORN_ITERS, tau=SINKHORN_TAU):
            Z = logits / tau
            u0 = jnp.zeros(Z.shape[:-1], Z.dtype)
            v0 = jnp.zeros_like(u0)

            def step(carry, _):
                u, v = carry
                u = -jax.nn.logsumexp(Z + v[..., None, :], axis=-1)
                v = -jax.nn.logsumexp(Z + u[..., :, None], axis=-2)
                return ((u, v), None)
            (u, v), _ = jax.lax.scan(step, (u0, v0), None, length=num_iters)
            return jnp.exp(Z + u[..., :, None] + v[..., None, :])
        B, T, nC = x.shape
        n = N_STREAMS
        C = nC // n
        x_norm = x * jax.lax.rsqrt(jnp.mean(x * x, axis=-1, keepdims=True) + RMS_EPS)
        H_res_logits = (x_norm @ W_res.T).reshape(B, T, n, n) + H_res_base
        H_pre_logits = x_norm @ W_pre.T + H_pre_base
        H_post_logits = x_norm @ W_post.T + H_post_base
        H_res = sinkhorn_log(H_res_logits)
        H_pre = jax.nn.softmax(H_pre_logits, axis=-1)
        H_post = jax.nn.softmax(H_post_logits, axis=-1)
        g = jax.nn.sigmoid(gate)[0]
        I = jnp.eye(n, dtype=H_res.dtype)
        H_res = (1.0 - g) * I + g * H_res
        x_streams = x.reshape(B, T, n, C)
        x_pre = jnp.einsum('btnc,btn->btc', x_streams, H_pre)
        y = x_pre @ W_branch
        x_mixed = jnp.einsum('btij,btjc->btic', H_res, x_streams)
        y_distributed = jnp.einsum('btc,btn->btnc', y, H_post)
        return (x_mixed + y_distributed).reshape(B, T, nC)
    x = x + _L0_xattn_ref(_layernorm(x, axis=-1), ctx_4096, ctx_4096, L0_xattn_Wq, L0_xattn_Wk, L0_xattn_Wv, L0_xattn_Wo, L0_xattn_bo, L0_xattn_g)
    x = x + _L0_ffn_ref(_layernorm(x, axis=-1), L0_ffn_W_res, L0_ffn_W_pre, L0_ffn_W_post, L0_ffn_H_res_base, L0_ffn_H_pre_base, L0_ffn_H_post_base, L0_ffn_gate, L0_ffn_W_branch)
    return x

_drawn_inputs = setup_inputs


def setup_inputs(seed=0):
    import zlib

    import numpy as np

    out = dict(_drawn_inputs(seed))
    spreads = {'L0_xattn_g': (1.0, 0.2), 'L0_ffn_H_post_base': (0.0, 0.8)}
    factors = {}
    for name, (base, spread) in spreads.items():
        noise = np.random.default_rng([zlib.crc32(name.encode()), seed]).standard_normal(out[name].shape)
        drawn = base * np.exp(spread * noise) if base else spread * noise
        out[name] = jnp.asarray(drawn.astype(out[name].dtype))
    for name, factor in factors.items():
        out[name] = (out[name] * factor).astype(out[name].dtype)
    return out
```

```python
from contextlib import ExitStack

import concourse.bass as bass
from concourse import mybir

ALU = mybir.AluOpType
ACT = mybir.ActivationFunctionType
AX_X = mybir.AxisListType.X
F32 = mybir.dt.float32
F32R = mybir.dt.float32r

P = 128
BANK = 512
LN_EPS = 1e-5
NORM_FLOOR = 1e-12
STREAMS = 4
SINKHORN_ITERS = 50
SINKHORN_TAU = 0.1
RMS_EPS = 1.1920929e-07
DIM_HEAD = 64
REFRESH = 10


class Queue:

    def __init__(self, engine):
        self.engine, self.steps, self.waited = engine, [], {}

    def __call__(self, after, signal, method, *args, **kwargs):
        for token in after:
            if token is not None:
                self.wait(*token)
        if signal is None:
            self.steps.append(lambda: method(*args, **kwargs))
            return None
        signal.value += signal.step
        self.steps.append(lambda: method(*args, **kwargs).then_inc(signal.handle, signal.step))
        return signal, signal.value

    def wait(self, signal, value):
        if self.waited.get(signal, 0) < value:
            self.waited[signal] = value
            self.steps.append(lambda: self.engine.wait_ge(signal.handle, value))

    def replay(self):
        for step in self.steps:
            step()


class Signal:

    def __init__(self, handle, step=1):
        self.handle, self.step, self.value = handle, step, 0


class Slot:

    def __init__(self, ap=None, h=None, l=None, sem=None):
        self.free, self.taken = [], False
        self.ap, self.h, self.l, self.sem = ap, h, l, sem

    def release(self, readers):
        self.free, self.taken = list(readers), False


class Ring:
    def __init__(self, slots):
        self.slots, self.n = slots, 0

    def take(self):
        slot = self.slots[self.n % len(self.slots)]
        self.n += 1
        assert not slot.taken
        slot.taken = True
        return slot


def xattn_ffn(nc, x, ctx, ctx_t, wq_t, wk_t, wv_t, wo_t, bo, g, w_maps_t, base, gate, w_branch, ln_spill, out):
    NB, C, N = x.shape
    HID = wq_t.shape[1]
    CT = C // P
    NT = N // P
    DT = HID // P
    HEADS = HID // DIM_HEAD
    NQ = N // BANK
    COLS = N // STREAMS
    KT = COLS // P
    MAPS = w_maps_t.shape[1]
    RES = STREAMS * STREAMS
    GROUP = 4
    T = GROUP * CT
    SCALE = DIM_HEAD ** -0.5

    stack = ExitStack()
    with stack:
        def sb(name, shape, dt=F32):
            return stack.enter_context(nc.sbuf_tensor(name, shape, dt))

        def signal(name, step=1):
            return Signal(stack.enter_context(nc.semaphore(name)), step)

        pe, dve, act = Queue(nc.tensor), Queue(nc.vector), Queue(nc.scalar)
        pool, sp = Queue(nc.gpsimd), Queue(nc.sync)

        s_const = signal("s_const")
        s_stage = [signal(f"s_stage{i}", 16) for i in range(2)]
        s_small = [signal(f"s_small{i}", 16) for i in range(4)]
        s_x = signal("s_x", 16)
        s_spill = signal("s_spill", 16)
        s_mixld = signal("s_mixld", 16)
        s_out = [signal(f"s_out{i}", 16) for i in range(2)]
        s_split_h = signal("s_split_h")
        s_split_l = signal("s_split_l")
        s_stat = signal("s_stat")
        s_pow = signal("s_pow")
        s_wq = signal("s_wq")
        s_wqh = signal("s_wqh")
        s_xh = signal("s_xh")
        s_xl = signal("s_xl")
        s_kmm = signal("s_kmm")
        s_kmax = signal("s_kmax")
        s_kexp = signal("s_kexp")
        s_tr = signal("s_tr")
        s_th = signal("s_th")
        s_tl = signal("s_tl")
        s_kc = signal("s_kc")
        s_chain = signal("s_chain")
        s_chd = signal("s_chd")
        s_cha = signal("s_cha")
        s_qmm = signal("s_qmm")
        s_qmax = signal("s_qmax")
        s_qexp = signal("s_qexp")
        s_qn = signal("s_qn")
        s_o = signal("s_o")
        s_ss = signal("s_ss")
        s_nrm = signal("s_nrm")
        s_on = signal("s_on")
        s_ot = signal("s_ot")
        s_x2 = signal("s_x2")
        s_ln = signal("s_ln")
        s_lg = signal("s_lg")
        s_lgd = signal("s_lgd")
        s_skd = signal("s_skd")
        s_ska = signal("s_ska")
        s_xp = signal("s_xp")
        s_xpa = signal("s_xpa")
        s_y = signal("s_y")
        s_ma = signal("s_ma")
        s_md = signal("s_md")

        wk = [sb(f"wk_{h}", [P, CT, HID], F32R) for h in "hl"]
        wv = [sb(f"wv_{h}", [P, CT, HID], F32R) for h in "hl"]
        wo = [sb(f"wo_{h}", [P, DT, C], F32R) for h in "hl"]
        wb = [sb(f"wb_{h}", [P, KT, COLS], F32R) for h in "hl"]
        wmap = sb("wmap", [P, NT * 2 * MAPS + P], F32R)
        wmap_tiles = wmap[:, 0:NT * 2 * MAPS].rearrange("p (t m) -> p t m", t=NT)
        wq = [sb(f"wq_{h}", [P, CT, HID], F32R) for h in "hl"]
        ident = sb("ident", [P, P])
        head_mask = sb("head_mask", [P, P])
        sel = sb("sel", [2 * MAPS, MAPS])
        bo_heads = sb("bo_heads", [P, C])
        base_rows = sb("base_rows", [P, MAPS])
        gcol = sb("gcol", [P, CT])
        gates = sb("gates", [P, 4])
        x_sb = sb("x_sb", [P, CT, N])
        ctx_hl = [sb(f"ctx_{h}", [P, CT, N], F32R) for h in "hl"]
        ctxt_hl = [sb(f"ctxt_{h}", [P, NT, C], F32R) for h in "hl"]
        k_exp = sb("k_exp", [P, N])
        stage = Ring([Slot(ap=sb(f"stage{i}", [P, 1024]), sem=s_stage[i]) for i in range(2)])
        halves = [Slot(h=sb(f"split{i}_h", [P, BANK], F32R), l=sb(f"split{i}_l", [P, BANK], F32R)) for i in range(3)]
        split, split_bg = Ring(halves[:2]), Ring(halves[2:])
        chain_hl = Slot(h=sb("chain_h", [P, 2 * P], F32R), l=sb("chain_l", [P, 2 * P], F32R))
        chain_raw = Slot(ap=sb("chain_raw", [P, C]))
        m_hl = [sb(f"m_{h}", [P, DT, C], F32R) for h in "hl"]
        q_sb = Ring([Slot(ap=sb(f"q_sb{i}", [P, HID])) for i in range(3)])
        xc = Ring([Slot(h=sb(f"xc{i}_h", [P, CT, 2 * P], F32R), l=sb(f"xc{i}_l", [P, CT, 2 * P], F32R)) for i in range(2)])
        on = Ring([Slot(ap=sb(f"on{i}", [P, C])) for i in range(2)])
        mix_ln = Slot(ap=sb("mix_ln", [P, N]))
        mix_out = Ring([Slot(ap=sb(f"mix_out{i}", [P, COLS]), sem=s_out[i]) for i in range(2)])
        squares = sb("squares", [P, C], mybir.dt.bfloat16)
        stats = sb("stats", [P, CT, NQ, 6])
        mean_var = sb("mean_var", [P, CT, 2])
        ln1 = sb("ln1", [P, CT, 3])
        powers = sb("powers", [P, 3, CT])
        qmax = sb("qmax", [P, 2, HEADS])
        qsum = sb("qsum", [P, 2, 2, HEADS])
        kmax = sb("kmax", [P, 2])
        ksum = sb("ksum", [P, NQ + 2])
        nrm = sb("nrm", [P, 2, 3, 2])
        ln2 = sb("ln2", [P, CT, 6])
        LT = NB * CT
        lg = sb("lg", [P, LT, MAPS])
        sd_all = sb("sd_all", [P, LT])
        mean_all = sb("mean_all", [P, LT])
        skz = sb("skz", [P, T, STREAMS, STREAMS])
        skp = sb("skp", [P, T, STREAMS, STREAMS])
        skw = sb("skw", [P, T, STREAMS, STREAMS])
        sku = sb("sku", [P, T, STREAMS])
        skv = sb("skv", [P, T, STREAMS])
        ska = sb("ska", [P, T, STREAMS])
        skb = sb("skb", [P, T, STREAMS])
        skr = sb("skr", [P, T, STREAMS])
        pre = sb("pre", [P, T, STREAMS])
        post = sb("post", [P, T, STREAMS])
        soft = sb("soft", [P, T, 2])

        big_t = stack.enter_context(nc.psum_tensor("big", [P, 4, BANK], F32))
        big = [Slot(ap=big_t[:, i, :]) for i in range(4)]
        tbank = Ring([Slot(ap=stack.enter_context(nc.psum_tensor(f"tbank{i}", [P, BANK], F32))) for i in range(2)])
        kc_bank = Slot(ap=stack.enter_context(nc.psum_tensor("kc_bank", [P, BANK], F32)))
        misc = Slot(ap=stack.enter_context(nc.psum_tensor("misc", [P, BANK], F32)))

        def f32(ap):
            return ap.bitcast(F32)

        def products(outp, left, right, after, sig, first=True, last=True):
            pairs = [(left[0], right[0]), (left[0], right[1]), (left[1], right[0])]
            token = None
            for i, (a, b) in enumerate(pairs):
                token = pe(after if i == 0 else (), sig if i == 2 else None,
                           nc.tensor.matmul, outp, a, b, start=(first and i == 0), stop=(last and i == 2))
            return token

        c0 = pool((), s_const, nc.gpsimd.memset, ident[:], 0.0)
        c_id = pool((c0,), s_const,
                    nc.gpsimd.affine_select, out=ident[:], in_=ident[:], compare_op=ALU.not_equal, fill=1.0, base=0, pattern=[[-1, P]], channel_multiplier=1)
        c1 = pool((), s_const, nc.gpsimd.memset, head_mask[:], 0.0)
        c1 = pool((c1,), s_const, nc.gpsimd.memset, head_mask[0:DIM_HEAD, 0:DIM_HEAD], SCALE)
        c_mask = pool((c1,), s_const, nc.gpsimd.memset, head_mask[DIM_HEAD:P, DIM_HEAD:P], SCALE)
        c2 = pool((), s_const, nc.gpsimd.memset, sel[:], 0.0)
        c2 = pool((c2,), s_const,
                  nc.gpsimd.affine_select, out=sel[:], in_=sel[:], compare_op=ALU.not_equal, fill=1.0, base=0, pattern=[[-1, MAPS]], channel_multiplier=1)
        c_sel = pool((c2,), s_const,
                     nc.gpsimd.affine_select, out=sel[:], in_=sel[:], compare_op=ALU.not_equal, fill=1.0, base=-MAPS, pattern=[[-1, MAPS]], channel_multiplier=1)
        c_w0 = pool((), s_const, nc.gpsimd.memset, f32(wmap[:]), 0.0)
        pool((), s_const, nc.gpsimd.memset, powers[:, 0, :], -0.5)
        c_pow = pool((), s_const, nc.gpsimd.memset, powers[:, 1, :], 0.5)

        small = [
            (bo_heads[:], bo.rearrange("(a c) -> a c", a=1).broadcast_to([P, C])),
            (base_rows[:], base.rearrange("(a m) -> a m", a=1).broadcast_to([P, MAPS])),
            (gcol[:], g),
            (gates[:, 0:1], gate.rearrange("(a c) -> a c", a=1).broadcast_to([P, 1])),
        ]
        landed = [sp((), s_small[i], nc.sync.dma_start, d, s) for i, (d, s) in enumerate(small)]
        c_bo = dve((landed[0],), s_stat, nc.vector.tensor_scalar, bo_heads[:], bo_heads[:], 1.0 / HEADS, None, ALU.mult)
        c_g = dve((landed[2],), s_stat, nc.vector.tensor_scalar, gcol[:], gcol[:], float(C) ** 0.5, None, ALU.mult)
        t = act((landed[3],), s_ska, nc.scalar.activation, gates[:, 1:2], gates[:, 0:1], ACT.Exp, scale=-1.0)
        t = dve((t,), s_stat, nc.vector.tensor_scalar, gates[:, 1:2], gates[:, 1:2], 1.0, None, ALU.add)
        t = dve((t,), s_stat, nc.vector.reciprocal, gates[:, 2:3], gates[:, 1:2])
        c_gate = dve((t,), s_stat, nc.vector.tensor_scalar, gates[:, 3:4], gates[:, 2:3], -1.0, 1.0, ALU.mult, ALU.add)

        def load_split(src, high, low, before=()):
            slot = stage.take()
            width = 1
            for n in src.shape[1:]:
                width *= n
            ap = slot.ap[:, 0:width]
            if len(src.shape) == 3:
                ap = ap.rearrange("p (a b) -> p a b", a=src.shape[1])
            t = sp(slot.free, slot.sem, nc.sync.dma_start, ap, src)
            th = act((t, *before), s_split_h, nc.scalar.copy, high, ap)
            tl = pool((t, th, *before), s_split_l, nc.gpsimd.tensor_tensor, low, ap, f32(high), ALU.subtract)
            slot.release([tl])
            return th, tl

        w_ready = {}
        w_ready["k"] = load_split(wk_t.rearrange("(t p) o -> p t o", p=P), wk[0][:], wk[1][:])
        w_ready["v"] = load_split(wv_t.rearrange("(t p) o -> p t o", p=P), wv[0][:], wv[1][:])
        w_ready["o"] = load_split(wo_t.rearrange("(t p) o -> p t o", p=P), wo[0][:], wo[1][:])
        for j in range(2):
            w_ready["b"] = load_split(w_branch.rearrange("(t p) o -> p t o", p=P)[:, 2 * j:2 * j + 2, :],
                                      wb[0][:, 2 * j:2 * j + 2, :], wb[1][:, 2 * j:2 * j + 2, :])
        w_ready["m"] = load_split(w_maps_t.rearrange("(t p) o -> p t o", p=P),
                                  wmap_tiles[:, :, 0:MAPS], wmap_tiles[:, :, MAPS:2 * MAPS], (c_w0,))

        ctx_free = [[] for _ in range(NQ)]
        ctxt_free = [[] for _ in range(NQ)]
        ctx_ready = [None] * NQ
        ctxt_ready = [None] * NQ

        def load_context(b):
            rows = ctx[b].rearrange("(t p) n -> p t n", p=P)
            for i in range(NQ):
                cols = slice(i * BANK, (i + 1) * BANK)
                ctx_ready[i] = load_split(rows[:, :, cols], ctx_hl[0][:, :, cols], ctx_hl[1][:, :, cols], ctx_free[i])
                yield
            cols_t = ctx_t[b].rearrange("(t p) c -> p t c", p=P)
            for i in range(NQ):
                nts = slice(i * NT // NQ, (i + 1) * NT // NQ)
                ctxt_ready[i] = load_split(cols_t[:, nts, :], ctxt_hl[0][:, nts, :], ctxt_hl[1][:, nts, :], ctxt_free[i])
                yield

        def transposed(sources, after):
            bank = tbank.take()
            for j, s in enumerate(sources):
                t = pe((*bank.free, *after, c_id) if j == 0 else (), s_tr if j == len(sources) - 1 else None,
                       nc.tensor.transpose, bank.ap[:, j * P:(j + 1) * P], s, ident[:])
            return bank, t

        def split_bank(bank, written, slot, width):
            th = act((written, *slot.free), s_th, nc.scalar.copy, slot.h[:, 0:width], bank.ap[:, 0:width])
            tl = dve((th, *slot.free), s_tl,
                     nc.vector.tensor_tensor, slot.l[:, 0:width], bank.ap[:, 0:width], f32(slot.h[:, 0:width]), ALU.subtract)
            bank.release([tl])
            return th, tl

        background = []

        def work(n=1):
            for _ in range(n):
                while background:
                    try:
                        next(background[0])
                        background.append(background.pop(0))
                        break
                    except StopIteration:
                        background.pop(0)

        def finish_background():
            while background:
                work()

        m_free = []
        m_ready = []
        kexp_free = [[] for _ in range(NQ)]
        ksum_free = [[]]

        def key_logits(dt):
            for i in range(NQ):
                cols = slice(i * BANK, (i + 1) * BANK)
                for ct in range(CT):
                    t = products(big[i].ap, [w[:, ct, dt * P:(dt + 1) * P] for w in wk],
                                 [c[:, ct, cols] for c in ctx_hl],
                                 (*big[i].free, *ctx_ready[i], *w_ready["k"]), s_kmm, ct == 0, ct == CT - 1)
                ctx_free[i] = [t]
            return t

        def key_softmax(written):
            tm = dve((written, *ksum_free[0]), s_kmax,
                     nc.vector.tensor_reduce, kmax[:, 0:1], big_t[:, :, :].rearrange("p a b -> p (a b)"), AX_X, ALU.max, negate=True)
            tokens = []
            for i in range(NQ):
                t = act((tm, *kexp_free[i], *ksum_free[0]), s_kexp,
                        nc.scalar.activation, k_exp[:, i * BANK:(i + 1) * BANK], big[i].ap, ACT.Exp, bias=kmax[:, 0:1], accum_out=ksum[:, i:i + 1])
                big[i].release([t])
                tokens.append(t)
            t = dve((t,), s_kmax, nc.vector.tensor_reduce, ksum[:, NQ:NQ + 1], ksum[:, 0:NQ], AX_X, ALU.add)
            t = dve((t,), s_kmax, nc.vector.reciprocal, ksum[:, NQ + 1:NQ + 2], ksum[:, NQ:NQ + 1])
            return tokens, t

        def key_context(dt, exps):
            pending = None
            per = NT // NQ

            def multiply(g, slot, split_tokens):
                for j in range(per):
                    nt = g * per + j
                    t = products(kc_bank.ap[:, 0:C], [slot.h[:, j * P:(j + 1) * P], slot.l[:, j * P:(j + 1) * P]],
                                 [c[:, nt, :] for c in ctxt_hl],
                                 (*split_tokens, *ctxt_ready[g], *kc_bank.free), s_kc, nt == 0, nt == NT - 1)
                slot.release([t])
                ctxt_free[g] = [t]
                return t

            for g in range(NQ):
                bank, t = transposed([k_exp[:, (g * per + j) * P:(g * per + j + 1) * P] for j in range(per)], (exps[g],))
                kexp_free[g] = [t]
                slot = split.take()
                tokens = split_bank(bank, t, slot, BANK)
                if pending:
                    multiply(*pending)
                work()
                pending = (g, slot, tokens)
            return multiply(*pending)

        def output_matrix(dt, kc_done, rsum):
            t = dve((kc_done, rsum, *chain_raw.free), s_chd,
                    nc.vector.tensor_scalar, chain_raw.ap[:, 0:C], kc_bank.ap[:, 0:C], ksum[:, NQ + 1:NQ + 2], None, ALU.mult)
            kc_bank.release([t])
            ksum_free[0] = [t]
            yield
            bank, t = transposed([chain_raw.ap[:, j * P:(j + 1) * P] for j in range(CT)], (t,))
            chain_raw.release([t])
            split_tokens = split_bank(bank, t, chain_hl, CT * P)
            yield
            bank = tbank.take()
            for ct in range(CT):
                t = products(bank.ap[:, 0:P], [w[:, ct, dt * P:(dt + 1) * P] for w in wv],
                             [chain_hl.h[:, ct * P:(ct + 1) * P], chain_hl.l[:, ct * P:(ct + 1) * P]],
                             (*bank.free, *split_tokens, *w_ready["v"]), s_chain, ct == 0, ct == CT - 1)
            td = dve((t, c_mask, *chain_raw.free), s_chd,
                     nc.vector.tensor_tensor, chain_raw.ap[:, 0:P], bank.ap[:, 0:P], head_mask[:], ALU.mult)
            bank.release([td])
            th = act((td, t), s_cha, nc.scalar.copy, chain_hl.h[:, 0:P], chain_raw.ap[:, 0:P])
            tl = dve((th, t), s_chd,
                     nc.vector.tensor_tensor, chain_hl.l[:, 0:P], chain_raw.ap[:, 0:P], f32(chain_hl.h[:, 0:P]), ALU.subtract)
            yield
            bank = tbank.take()
            t = products(bank.ap[:, 0:C], [chain_hl.h[:, 0:P], chain_hl.l[:, 0:P]], [w[:, dt, :] for w in wo],
                         (*bank.free, th, tl, *w_ready["o"]), s_chain)
            chain_hl.release([t])
            td = dve((t, tl, c_bo), s_chd,
                     nc.vector.tensor_tensor, chain_raw.ap[:, 0:C], bank.ap[:, 0:C], bo_heads[:], ALU.add)
            bank.release([td])
            th = act((td, *m_free), s_cha, nc.scalar.copy, m_hl[0][:, dt, :], chain_raw.ap[:, 0:C])
            tl = dve((th, *m_free), s_chd,
                     nc.vector.tensor_tensor, m_hl[1][:, dt, :], chain_raw.ap[:, 0:C], f32(m_hl[0][:, dt, :]), ALU.subtract)
            chain_raw.release([tl])
            m_ready.append(th)
            m_ready.append(tl)

        def keys(b):
            m_ready.clear()
            previous = chain = None
            for dt in range(DT + 1):
                if dt < DT:
                    written = key_logits(dt)
                if chain:
                    for _ in chain:
                        work()
                    chain = None
                if previous:
                    done = key_context(dt - 1, previous[0])
                    chain = output_matrix(dt - 1, done, previous[1])
                    next(chain)
                if dt < DT:
                    previous = key_softmax(written)
                else:
                    previous = None
            return chain

        x_free = []

        def row_stats(after):
            for ct in range(CT):
                for i in range(NQ):
                    t = dve(after, s_stat, nc.vector.bn_stats, stats[:, ct, i, :], x_sb[:, ct, i * BANK:(i + 1) * BANK])
            for ct in range(CT):
                u = dve((t,), s_stat,
                        nc.vector.bn_aggr, mean_var[:, ct, :], stats[:, ct, :, :].rearrange("p a b -> p (a b)"))
            return u

        xq = {}

        def query_prepare(b):
            t = sp(x_free, s_x, nc.sync.dma_start, x_sb[:], x[b].rearrange("(t p) n -> p t n", p=P))
            xq["x"] = t
            yield
            t = row_stats((t,))
            t = dve((t, *xq.get("ln1_free", ())), s_stat,
                    nc.vector.tensor_scalar, ln1[:, :, 0], mean_var[:, :, 1], LN_EPS, None, ALU.add)
            t2 = dve((t,), s_stat, nc.vector.tensor_scalar, ln1[:, :, 2], mean_var[:, :, 0], -1.0, None, ALU.mult)
            xq["mean"] = t2
            t = pool((t, c_pow), s_pow, nc.gpsimd.tensor_tensor, ln1[:, :, 1], ln1[:, :, 0], powers[:, 0, :], ALU.pow)
            yield
            tokens = []
            raw = stage.take()
            wq_raw = raw.ap.rearrange("p (t o) -> p t o", t=CT)
            c_wq = sp(raw.free, raw.sem, nc.sync.dma_start, wq_raw, wq_t.rearrange("(t p) o -> p t o", p=P))
            for ct in range(CT):
                th = act((t, c_wq, *xq.get("wq_free", ())), s_wqh,
                         nc.scalar.activation, wq[0][:, ct, :], wq_raw[:, ct, :], ACT.Copy, scale=ln1[:, ct, 1:2])
                tl = dve((th,), s_wq,
                         nc.vector.scalar_tensor_tensor, out=wq[1][:, ct, :], in0=wq_raw[:, ct, :], scalar=ln1[:, ct, 1:2], in1=f32(wq[0][:, ct, :]), op0=ALU.mult, op1=ALU.subtract)
                tokens += [th, tl]
            raw.release([tl])
            xq["wq"] = tokens

        def center(pair):
            slot = xc.take()
            cols = slice(pair * 2 * P, (pair + 1) * 2 * P)
            tokens = []
            for ct in range(CT):
                th = act((xq["mean"], *slot.free), s_xh,
                         nc.scalar.activation, slot.h[:, ct, :], x_sb[:, ct, cols], ACT.Identity, bias=ln1[:, ct, 2:3])
                tl = dve((th, *slot.free), s_xl,
                         nc.vector.scalar_tensor_tensor, out=slot.l[:, ct, :], in0=x_sb[:, ct, cols], scalar=ln1[:, ct, 2:3], in1=f32(slot.h[:, ct, :]), op0=ALU.add, op1=ALU.subtract)
                tokens += [th, tl]
            xq[pair] = (slot, tokens, th, tl)

        qt = {}

        def query_logits(i):
            slot, tokens = xq[i // 2][:2]
            cols = slice((i % 2) * P, (i % 2 + 1) * P)
            bank = big[i % 2]
            for ct in range(CT):
                t = products(bank.ap, [slot.h[:, ct, cols], slot.l[:, ct, cols]], [w[:, ct, :] for w in wq],
                             (*bank.free, *tokens, *xq["wq"]), s_qmm, ct == 0, ct == CT - 1)
            if i % 2:
                slot.release([t])
            xq["wq_free"] = xq["ln1_free"] = [t]
            qt[i] = t

        def query_softmax(i):
            bank, buf, k = big[i % 2], q_sb.take(), i % 2
            heads = "p (h d) -> p h d"
            t = dve((qt[i],), s_qmax,
                    nc.vector.tensor_reduce, qmax[:, k, :], bank.ap.rearrange(heads, d=DIM_HEAD), AX_X, ALU.max)
            t = dve((t, *buf.free), s_qmax,
                    nc.vector.tensor_tensor, buf.ap[:].rearrange(heads, d=DIM_HEAD), bank.ap.rearrange(heads, d=DIM_HEAD), qmax[:, k, :].unsqueeze(2).broadcast_to([P, HEADS, DIM_HEAD]), ALU.subtract)
            bank.release([t])
            qt[i] = (buf, act((t,), s_qexp, nc.scalar.activation, buf.ap[:], buf.ap[:], ACT.Exp))

        def query_normalise(i):
            buf, t = qt[i]
            k = i % 2
            heads = "p (h d) -> p h d"
            t = dve((t,), s_qmax,
                    nc.vector.tensor_reduce, qsum[:, k, 0, :], buf.ap[:].rearrange(heads, d=DIM_HEAD), AX_X, ALU.add)
            t = dve((t, *qt.get(("rfree", k), ())), s_qmax, nc.vector.reciprocal, qsum[:, k, 1, :], qsum[:, k, 0, :])
            t = pool((t,), s_qn,
                     nc.gpsimd.tensor_tensor, buf.ap[:].rearrange(heads, d=DIM_HEAD), buf.ap[:].rearrange(heads, d=DIM_HEAD), qsum[:, k, 1, :].unsqueeze(2).broadcast_to([P, HEADS, DIM_HEAD]), ALU.mult)
            qt["rfree", k] = [t]
            qt[i] = (buf, t)

        def query_transpose(i):
            buf, t = qt[i]
            bank, t = transposed([buf.ap[:, j * P:(j + 1) * P] for j in range(DT)], (t,))
            buf.release([t])
            slot = split.take()
            qt[i] = (slot, split_bank(bank, t, slot, HID))

        def attention_out(i):
            slot, tokens = qt[i]
            bank = big[2 + (i // 2) % 2]
            half = slice((i % 2) * C, (i % 2 + 1) * C)
            for dt in range(DT):
                t = products(bank.ap[:, half], [slot.h[:, dt * P:(dt + 1) * P], slot.l[:, dt * P:(dt + 1) * P]],
                             [m[:, dt, :] for m in m_hl], ((*bank.free,) if i % 2 == 0 else ()) + (*tokens, *m_ready), s_o, dt == 0, dt == DT - 1)
            slot.release([t])
            m_free[:] = [t]
            qt[i] = t

        def normalise_pair(p):
            bank, k = big[2 + p % 2], p % 2
            t = None
            for j in range(2):
                t = act((qt[2 * p + 1], t, *qt.get(("nfree", k), ()), qt.get("sq")), s_ss,
                        nc.scalar.activation, squares[:], bank.ap[:, j * C:(j + 1) * C], ACT.Square, accum_out=nrm[:, k, 0, j:j + 1])
                qt["sq"] = t
            t = pool((t, c_pow), s_pow,
                     nc.gpsimd.tensor_tensor, nrm[:, k, 1, :], nrm[:, k, 0, :], powers[:, 1, 0:2], ALU.pow)
            t = dve((t,), s_nrm, nc.vector.tensor_scalar, nrm[:, k, 1, :], nrm[:, k, 1, :], NORM_FLOOR, None, ALU.max)
            qt["norm", p] = dve((t,), s_nrm, nc.vector.reciprocal, nrm[:, k, 2, :], nrm[:, k, 1, :])

        def scale_pair(p):
            bank, k = big[2 + p % 2], p % 2
            for j in range(2):
                buf = on.take()
                t = act((qt["norm", p], *buf.free), s_on,
                        nc.scalar.activation, buf.ap[:], bank.ap[:, j * C:(j + 1) * C], ACT.Copy, scale=nrm[:, k, 2, j:j + 1])
                for ct in range(CT):
                    off = ct * 2 * P + j * P
                    u = pe((t, *kc_bank.free), s_ot,
                           nc.tensor.transpose, kc_bank.ap[:, off:off + P], buf.ap[:, ct * P:(ct + 1) * P], ident[:])
                buf.release([u])
            bank.release([t])
            qt["nfree", k] = [t]
            for ct in range(CT):
                cols = slice(p * 2 * P, (p + 1) * 2 * P)
                v = dve((u, c_g, *xq[p][1]), s_x2,
                        nc.vector.scalar_tensor_tensor, out=x_sb[:, ct, cols], in0=kc_bank.ap[:, ct * 2 * P:(ct + 1) * 2 * P], scalar=gcol[:, ct:ct + 1], in1=x_sb[:, ct, cols], op0=ALU.mult, op1=ALU.add)
            kc_bank.release([v])
            xq["x2"] = v

        def queries(b, chain):
            LAG_T, LAG_O, LAG_N, LAG_S = 2, 3, 4, 5
            center(0)
            for i in range(NT + LAG_S + 1):
                if i < NT:
                    if i % 2 == 0 and i // 2 + 1 < NT // 2:
                        center(i // 2 + 1)
                    query_logits(i)
                    query_softmax(i)
                if chain:
                    if next(chain, "end") == "end":
                        chain = None
                if 1 <= i <= NT:
                    query_normalise(i - 1)
                if LAG_T <= i < NT + LAG_T:
                    query_transpose(i - LAG_T)
                if LAG_O <= i < NT + LAG_O:
                    while chain and i == LAG_O:
                        if next(chain, "end") == "end":
                            chain = None
                    attention_out(i - LAG_O)
                j = i - LAG_N
                if 0 <= j < NT and j % 2 == 1:
                    normalise_pair(j // 2)
                j = i - LAG_S
                if 0 <= j < NT and j % 2 == 1:
                    scale_pair(j // 2)
                work()

        def normalise_rows(b):
            t = row_stats((xq["x2"],))
            s = dve((t, *xq.get("ln2_free", ())), s_stat,
                    nc.vector.tensor_scalar, ln2[:, :, 0], mean_var[:, :, 1], LN_EPS, None, ALU.add)
            m = dve((t,), s_stat, nc.vector.tensor_copy, mean_all[:, b * CT:(b + 1) * CT], mean_var[:, :, 0])
            r = pool((s, c_pow), s_pow, nc.gpsimd.tensor_tensor, ln2[:, :, 1], ln2[:, :, 0], powers[:, 0, :], ALU.pow)
            d = pool((s,), s_pow,
                     nc.gpsimd.tensor_tensor, sd_all[:, b * CT:(b + 1) * CT], ln2[:, :, 0], powers[:, 1, :], ALU.pow)
            u = dve((r,), s_stat,
                    nc.vector.scalar_tensor_tensor, out=ln2[:, :, 2], in0=mean_var[:, :, 0], scalar=-1.0, in1=ln2[:, :, 1], op0=ALU.mult, op1=ALU.mult)
            w = dve((r,), s_stat, nc.vector.tensor_tensor, ln2[:, :, 3], ln2[:, :, 1], ln2[:, :, 1], ALU.mult)
            w = dve((w,), s_stat, nc.vector.tensor_tensor, ln2[:, :, 4], ln2[:, :, 3], mean_var[:, :, 1], ALU.mult)
            w = dve((w,), s_stat, nc.vector.tensor_scalar, ln2[:, :, 3], ln2[:, :, 4], RMS_EPS, None, ALU.add)
            w = pool((w,), s_pow, nc.gpsimd.tensor_tensor, ln2[:, :, 5], ln2[:, :, 3], powers[:, 0, :], ALU.pow)
            yield
            lns = []
            for ct in range(CT):
                lns.append(act((u, xq["x2"]), s_ln,
                               nc.scalar.activation, x_sb[:, ct, :], x_sb[:, ct, :], ACT.Identity, bias=ln2[:, ct, 2:3], scale=ln2[:, ct, 1:2]))
            spilled = sp(lns, s_spill, nc.sync.dma_start, ln_spill[b].rearrange("(t p) n -> p t n", p=P), x_sb[:])
            yield
            per = BANK // C

            def multiply(i, slot, tokens):
                for j in range(per):
                    nt = i * per + j
                    for h, half in enumerate((slot.h, slot.l)):
                        t = pe((*misc.free, *tokens, *w_ready["m"]), s_lg,
                               nc.tensor.matmul, misc.ap[:, 0:C], wmap[:, nt * 2 * MAPS:nt * 2 * MAPS + P], half[:, j * C:(j + 1) * C], start=(nt == 0 and h == 0), stop=(nt == NT - 1 and h == 1))
                slot.release([t])
                return t

            for i in range(NT // per):
                bank, t = transposed([x_sb[:, ct, (i * per + j) * P:(i * per + j + 1) * P] for j in range(per) for ct in range(CT)], lns)
                slot = split_bg.take()
                tokens = split_bank(bank, t, slot, BANK)
                xq["tr"] = t
                yield
                done = multiply(i, slot, tokens)
            x_free[:] = [spilled, xq["tr"]]
            buf = on.take()
            map_sb = buf.ap[0:2 * MAPS, :]
            t = dve((done, *buf.free), s_lgd, nc.vector.tensor_copy, map_sb, misc.ap[0:2 * MAPS, 0:C])
            misc.release([t])
            bank = tbank.take()
            for ct in range(CT):
                u = pe((*bank.free, t, c_sel), s_lg,
                       nc.tensor.matmul, bank.ap[:, ct * MAPS:(ct + 1) * MAPS], map_sb[:, ct * P:(ct + 1) * P], sel[:], start=True, stop=True)
            buf.release([u])
            for ct in range(CT):
                v = dve((u, w, landed[1]), s_lgd,
                        nc.vector.scalar_tensor_tensor, out=lg[:, b * CT + ct, :], in0=bank.ap[:, ct * MAPS:(ct + 1) * MAPS], scalar=ln2[:, ct, 5:6], in1=base_rows[:], op0=ALU.mult, op1=ALU.add)
            bank.release([v])
            xq["ln2_free"] = [v, lns[-1]]
            xq["lg", b] = v
            xq["spilled", b] = [spilled, d, m]

        sk = {"free": []}

        def sinkhorn(grp):
            tiles = slice(grp * T, (grp + 1) * T)
            lgs = [xq["lg", b] for b in range(grp * GROUP, (grp + 1) * GROUP)]

            def over_j(v):
                return v[:].unsqueeze(2).broadcast_to([P, T, STREAMS, STREAMS])

            def over_i(v):
                return v[:].unsqueeze(3).broadcast_to([P, T, STREAMS, STREAMS])

            def by_column(m):
                return m[:].rearrange("p t i j -> p t j i")

            def D(after, method, *args, **kwargs):
                return dve(after, s_skd, method, *args, **kwargs)

            def A(after, method, *args, **kwargs):
                return act(after, s_ska, method, *args, **kwargs)

            t = D([*lgs, *sk["free"]],
                  nc.vector.tensor_scalar, skz[:].rearrange("p t i j -> p t (i j)"), lg[:, tiles, 0:RES], 1.0 / SINKHORN_TAU, None, ALU.mult)

            def negative_lse(target, m, spread, t, first):
                t = D([t], nc.vector.tensor_reduce, skr[:], m, AX_X, ALU.max)
                t = D([t], nc.vector.tensor_tensor, skp[:], skw[:] if not first else skz[:], spread(skr), ALU.subtract)
                t = A([t], nc.scalar.activation, skp[:], skp[:], ACT.Exp)
                t = D([t], nc.vector.tensor_reduce, ska[:], skp[:] if spread is over_i else by_column(skp), AX_X, ALU.add)
                t = A([t], nc.scalar.activation, ska[:], ska[:], ACT.Ln)
                return D([t],
                         nc.vector.scalar_tensor_tensor, out=target[:], in0=ska[:], scalar=-1.0, in1=skr[:], op0=ALU.mult, op1=ALU.subtract)

            t = negative_lse(sku, skz[:], over_i, t, True)
            yield
            t = D([t], nc.vector.tensor_tensor, skw[:], skz[:], over_i(sku), ALU.add)
            t = negative_lse(skv, by_column(skw), over_j, t, False)
            yield
            done = 1
            while True:
                t = D([t], nc.vector.tensor_tensor, skw[:], skz[:], over_i(sku), ALU.add)
                t = D([t], nc.vector.tensor_tensor, skw[:], skw[:], over_j(skv), ALU.add)
                t = A([t], nc.scalar.activation, skp[:], skw[:], ACT.Exp)
                if done == SINKHORN_ITERS:
                    break
                rounds = min(REFRESH, SINKHORN_ITERS - done)
                for r in range(rounds):
                    if r:
                        t = D([t], nc.vector.tensor_tensor, skw[:], skp[:], over_j(skb), ALU.mult)
                    m = skw if r else skp
                    t = D([t], nc.vector.tensor_reduce, skr[:], m[:], AX_X, ALU.add)
                    t = D([t], nc.vector.reciprocal, ska[:], skr[:])
                    t = D([t], nc.vector.tensor_tensor, skw[:], skp[:], over_i(ska), ALU.mult)
                    t = D([t], nc.vector.tensor_reduce, skr[:], by_column(skw), AX_X, ALU.add)
                    t = D([t], nc.vector.reciprocal, skb[:], skr[:])
                    yield
                done += rounds
                for scaling, potential in ((ska, sku), (skb, skv)):
                    t = A([t], nc.scalar.activation, skr[:], scaling[:], ACT.Ln)
                    t = D([t], nc.vector.tensor_tensor, potential[:], potential[:], skr[:], ALU.add)
            t = D([t, c_gate], nc.vector.tensor_scalar, skp[:], skp[:], gates[:, 2:3], None, ALU.mult)
            diagonal = skp[:].rearrange("p t i j -> p t (i j)")[:, :, 0:RES:STREAMS + 1]
            t = D([t, *[tok for b in range(grp * GROUP, (grp + 1) * GROUP) for tok in xq["spilled", b][1:]]],
                  nc.vector.scalar_tensor_tensor, out=diagonal, in0=diagonal, scalar=gates[:, 3:4], in1=sd_all[:, tiles].unsqueeze(2).broadcast_to([P, T, STREAMS]), op0=ALU.add, op1=ALU.add)
            for k, target in enumerate((pre, post)):
                cols = slice(RES + k * STREAMS, RES + (k + 1) * STREAMS)
                wide = [P, T, STREAMS]
                t = D([t], nc.vector.tensor_reduce, soft[:, :, 0], lg[:, tiles, cols], AX_X, ALU.max)
                t = D([t],
                      nc.vector.tensor_tensor, target[:], lg[:, tiles, cols], soft[:, :, 0].unsqueeze(2).broadcast_to(wide), ALU.subtract)
                t = A([t], nc.scalar.activation, target[:], target[:], ACT.Exp)
                t = D([t], nc.vector.tensor_reduce, soft[:, :, 0], target[:], AX_X, ALU.add)
                t = D([t], nc.vector.reciprocal, soft[:, :, 1], soft[:, :, 0])
                t = D([t],
                      nc.vector.tensor_tensor, target[:], target[:], soft[:, :, 1].unsqueeze(2).broadcast_to(wide), ALU.mult)
            sk["done"] = t
            yield

        def mix(grp):
            free = []
            for tile in range(T):
                b, ct = grp * GROUP + tile // CT, tile % CT
                tok = grp * T + tile
                ln = mix_ln.ap
                t = sp((xq["spilled", b][0], *mix_ln.free), s_mixld,
                       nc.sync.dma_start, ln[:], ln_spill[b, ct * P:(ct + 1) * P, :])
                stream = [ln[:, j * COLS:(j + 1) * COLS] for j in range(STREAMS)]
                yield
                buf = q_sb.take()
                u = act((t, sk["done"], *buf.free), s_xpa,
                        nc.scalar.activation, buf.ap[:], stream[0], ACT.Copy, scale=pre[:, tile, 0:1])
                for j in range(1, STREAMS):
                    u = dve((u,), s_xp,
                            nc.vector.scalar_tensor_tensor, out=buf.ap[:], in0=stream[j], scalar=pre[:, tile, j:j + 1], in1=buf.ap[:], op0=ALU.mult, op1=ALU.add)
                bank, u = transposed([buf.ap[:, j * P:(j + 1) * P] for j in range(KT)], (u,))
                buf.release([u])
                slot = split_bg.take()
                tokens = split_bank(bank, u, slot, BANK)
                yield
                for k in range(KT):
                    y = products(misc.ap[:, 0:COLS], [slot.h[:, k * P:(k + 1) * P], slot.l[:, k * P:(k + 1) * P]],
                                 [w[:, k, :] for w in wb], (*misc.free, *tokens, *w_ready["b"]), s_y, k == 0, k == KT - 1)
                slot.release([y])
                yield
                for i in range(STREAMS):
                    o = mix_out.take()
                    v = act((t, *o.free, sk["done"]), s_ma,
                            nc.scalar.activation, o.ap[:], stream[0], ACT.Identity, bias=mean_all[:, tok:tok + 1], scale=skp[:, tile, i, 0:1])
                    for j in range(1, STREAMS):
                        v = dve((v,), s_md,
                                nc.vector.scalar_tensor_tensor, out=o.ap[:], in0=stream[j], scalar=skp[:, tile, i, j:j + 1], in1=o.ap[:], op0=ALU.mult, op1=ALU.add)
                    v = dve((v, y), s_md,
                            nc.vector.scalar_tensor_tensor, out=o.ap[:], in0=misc.ap[:, 0:COLS], scalar=post[:, tile, i:i + 1], in1=o.ap[:], op0=ALU.mult, op1=ALU.add)
                    w = sp((v,), o.sem, nc.sync.dma_start, out[b, ct * P:(ct + 1) * P, i * COLS:(i + 1) * COLS], o.ap[:])
                    o.release([w])
                    if i % 2:
                        yield
                misc.release([v])
                mix_ln.release([v])
            sk["free"] = [v]

        def context_of(b):
            for _ in load_context(b):
                pass

        def after_batch(b):
            yield from normalise_rows(b)
            if b + 1 < NB:
                yield from query_prepare(b + 1)

        def group_work(grp):
            yield from sinkhorn(grp)
            yield from mix(grp)

        context_of(0)
        for _ in query_prepare(0):
            pass
        for b in range(NB):
            chain = keys(b)
            finish_background()
            if b + 1 < NB:
                background.append(load_context(b + 1))
            queries(b, chain)
            finish_background()
            background.append(after_batch(b))
            if b % GROUP == GROUP - 1:
                finish_background()
                background.append(group_work(b // GROUP))
        finish_background()
        for s in (*s_out, s_spill):
            sp.wait(s, s.value)

        block = stack.enter_context(nc.Block())

        @block.sync
        def _(e):
            sp.replay()

        @block.tensor
        def _(e):
            pe.replay()

        @block.vector
        def _(e):
            dve.replay()

        @block.scalar
        def _(e):
            act.replay()

        @block.gpsimd
        def _(e):
            pool.replay()


def kernel(x, ctx_4096, L0_xattn_Wq, L0_xattn_Wk, L0_xattn_Wv, L0_xattn_Wo, L0_xattn_bo, L0_xattn_g, L0_ffn_W_res,
           L0_ffn_W_pre, L0_ffn_W_post, L0_ffn_H_res_base, L0_ffn_H_pre_base, L0_ffn_H_post_base, L0_ffn_gate, L0_ffn_W_branch):
    import numpy as np
    import concourse.bacc as bacc
    from concourse.bass_utils import run_bass_kernel_spmd

    host = {
        "x": x,
        "ctx": ctx_4096,
        "ctx_t": np.swapaxes(ctx_4096, 1, 2),
        "wq_t": np.transpose(L0_xattn_Wq),
        "wk_t": np.transpose(L0_xattn_Wk),
        "wv_t": np.transpose(L0_xattn_Wv),
        "wo_t": np.transpose(L0_xattn_Wo),
        "bo": L0_xattn_bo,
        "g": np.transpose(np.reshape(L0_xattn_g, (-1, P))),
        "w_maps_t": np.transpose(np.concatenate([L0_ffn_W_res, L0_ffn_W_pre, L0_ffn_W_post], axis=0)),
        "base": np.concatenate([np.reshape(L0_ffn_H_res_base, (-1,)), L0_ffn_H_pre_base, L0_ffn_H_post_base]),
        "gate": L0_ffn_gate,
        "w_branch": L0_ffn_W_branch,
    }
    nc = bacc.Bacc("TRN2", target_bir_lowering=False, num_devices=1)
    arrays, aps = {}, []
    for name, a in host.items():
        a = np.ascontiguousarray(a)
        arrays[f"in_{name}"] = a
        aps.append(nc.dram_tensor(f"in_{name}", a.shape, mybir.dt.from_np(a.dtype), kind="ExternalInput").ap())
    shape = tuple(x.shape)
    aps.append(nc.dram_tensor("ln_spill", shape, F32, kind="Internal").ap())
    aps.append(nc.dram_tensor("out_0", shape, F32, kind="ExternalOutput").ap())
    xattn_ffn(nc, *aps)
    r = run_bass_kernel_spmd(nc, [arrays], core_ids=[0])
    return r.results[0]["out_0"]
```

```python
from contextlib import ExitStack

import concourse.bass as bass
from concourse import mybir

ALU = mybir.AluOpType
ACT = mybir.ActivationFunctionType
AX_X = mybir.AxisListType.X
F32 = mybir.dt.float32
F32R = mybir.dt.float32r

P = 128
BANK = 512
LN_EPS = 1e-5
NORM_FLOOR = 1e-12
STREAMS = 4
SINKHORN_ITERS = 50
SINKHORN_TAU = 0.1
RMS_EPS = 1.1920929e-07
DIM_HEAD = 64
REFRESH = 10


class Queue:

    def __init__(self, engine):
        self.engine, self.steps, self.waited = engine, [], {}

    def __call__(self, after, signal, method, *args, **kwargs):
        for token in after:
            if token is not None:
                self.wait(*token)
        if signal is None:
            self.steps.append(lambda: method(*args, **kwargs))
            return None
        signal.value += signal.step
        self.steps.append(lambda: method(*args, **kwargs).then_inc(signal.handle, signal.step))
        return signal, signal.value

    def wait(self, signal, value):
        if self.waited.get(signal, 0) < value:
            self.waited[signal] = value
            self.steps.append(lambda: self.engine.wait_ge(signal.handle, value))

    def replay(self):
        for step in self.steps:
            step()


class Signal:

    def __init__(self, handle, step=1):
        self.handle, self.step, self.value = handle, step, 0


class Slot:

    def __init__(self, ap=None, h=None, l=None, sem=None):
        self.free, self.taken = [], False
        self.ap, self.h, self.l, self.sem = ap, h, l, sem

    def take(self):
        assert not self.taken
        self.taken = True
        return self

    def release(self, readers):
        self.free, self.taken = list(readers), False


class Ring:
    def __init__(self, slots):
        self.slots, self.n = slots, 0

    def take(self):
        assert self.ready()
        while self.slots[self.n % len(self.slots)].taken:
            self.n += 1
        self.n += 1
        return self.slots[(self.n - 1) % len(self.slots)].take()

    def ready(self):
        return not all(slot.taken for slot in self.slots)


def xattn_ffn(nc, x, ctx, ctx_t, wq_t, wk_t, wv_t, wo_t, bo, g, w_maps_t, base, gate, w_branch, ln_spill, out):
    NB, C, N = x.shape
    HID = wq_t.shape[1]
    CT = C // P
    NT = N // P
    DT = HID // P
    HEADS = HID // DIM_HEAD
    NQ = N // BANK
    COLS = N // STREAMS
    KT = COLS // P
    MAPS = w_maps_t.shape[1]
    RES = STREAMS * STREAMS
    GROUPS = [4, 4, 4, 4]
    TMAX = max(GROUPS) * CT
    LOGITS = 2 * TMAX
    SCALE = DIM_HEAD ** -0.5

    stack = ExitStack()
    with stack:
        def sb(name, shape, dt=F32):
            return stack.enter_context(nc.sbuf_tensor(name, shape, dt))

        def signal(name, step=1):
            return Signal(stack.enter_context(nc.semaphore(name)), step)

        pe, dve, act = Queue(nc.tensor), Queue(nc.vector), Queue(nc.scalar)
        pool, sp = Queue(nc.gpsimd), Queue(nc.sync)

        s_const = signal("s_const")
        s_stage = [signal(f"s_stage{i}", 16) for i in range(2)]
        s_small = [signal(f"s_small{i}", 16) for i in range(4)]
        s_x = signal("s_x", 16)
        s_spill = signal("s_spill", 16)
        s_mixld = [signal(f"s_mixld{i}", 16) for i in range(1 + x.shape[1] // P)]
        s_out = [signal(f"s_out{i}", 16) for i in range(2)]
        s_split_h = signal("s_split_h")
        s_split_l = signal("s_split_l")
        s_stat = signal("s_stat")
        s_pow = signal("s_pow")
        s_wq = signal("s_wq")
        s_wqh = signal("s_wqh")
        s_xh = signal("s_xh")
        s_xl = signal("s_xl")
        s_kmm = signal("s_kmm")
        s_kmax = signal("s_kmax")
        s_kexp = signal("s_kexp")
        s_tr = signal("s_tr")
        s_th = signal("s_th")
        s_tl = signal("s_tl")
        s_kc = signal("s_kc")
        s_chain = signal("s_chain")
        s_chd = signal("s_chd")
        s_cha = signal("s_cha")
        s_qmm = signal("s_qmm")
        s_qmax = signal("s_qmax")
        s_qhalf = signal("s_qhalf")
        s_qexp = signal("s_qexp")
        s_qn = signal("s_qn")
        s_o = signal("s_o")
        s_ss = signal("s_ss")
        s_nrm = signal("s_nrm")
        s_on = signal("s_on")
        s_ot = signal("s_ot")
        s_x2 = signal("s_x2")
        s_ln = signal("s_ln")
        s_lg = signal("s_lg")
        s_lgd = signal("s_lgd")
        s_skd = signal("s_skd")
        s_ska = signal("s_ska")
        s_xp = signal("s_xp")
        s_xpa = signal("s_xpa")
        s_y = signal("s_y")
        s_ya = signal("s_ya")
        s_ma = signal("s_ma")
        s_md = signal("s_md")

        wk = [sb(f"wk_{h}", [P, CT, HID], F32R) for h in "hl"]
        wv = [sb(f"wv_{h}", [P, CT, HID], F32R) for h in "hl"]
        wo = [sb(f"wo_{h}", [P, DT, C], F32R) for h in "hl"]
        wb = [sb(f"wb_{h}", [P, KT, COLS], F32R) for h in "hl"]
        wmap = sb("wmap", [P, NT * 2 * MAPS + P], F32R)
        wmap_tiles = wmap[:, 0:NT * 2 * MAPS].rearrange("p (t m) -> p t m", t=NT)
        wq = [sb(f"wq_{h}", [P, CT, HID], F32R) for h in "hl"]
        ident = sb("ident", [P, P])
        head_mask = sb("head_mask", [P, P])
        sel = sb("sel", [2 * MAPS, MAPS])
        bo_heads = sb("bo_heads", [P, C])
        base_rows = sb("base_rows", [P, MAPS])
        gcol = sb("gcol", [P, CT])
        gates = sb("gates", [P, 4])
        x_sb = sb("x_sb", [P, CT, N])
        ctx_hl = [sb(f"ctx_{h}", [P, CT, N], F32R) for h in "hl"]
        ctxt_hl = [sb(f"ctxt_{h}", [P, NT, C], F32R) for h in "hl"]
        k_exp = sb("k_exp", [P, N])
        stage = Ring([Slot(ap=sb(f"stage{i}", [P, 1024]), sem=s_stage[i]) for i in range(2)])
        halves = [Slot(h=sb(f"split{i}_h", [P, BANK], F32R), l=sb(f"split{i}_l", [P, BANK], F32R)) for i in range(3)]
        split, split_bg = Ring(halves[:2]), Ring(halves[2:])
        chain_hl = Slot(h=sb("chain_h", [P, 2 * P], F32R), l=sb("chain_l", [P, 2 * P], F32R))
        chain_raw = Slot(ap=sb("chain_raw", [P, C]))
        m_hl = [sb(f"m_{h}", [P, DT, C], F32R) for h in "hl"]
        q_sb = Ring([Slot(ap=sb(f"q_sb{i}", [P, HID])) for i in range(2)])
        xc = Ring([Slot(h=sb(f"xc{i}_h", [P, CT, 2 * P], F32R), l=sb(f"xc{i}_l", [P, CT, 2 * P], F32R)) for i in range(2)])
        on = Ring([Slot(ap=sb(f"on{i}", [P, C])) for i in range(2)])
        y_sb = Slot(ap=sb("y_sb", [P, COLS]))
        mix_ln = Ring([Slot(ap=sb("mix_ln", [P, N])[:], sem=s_mixld[0])])
        mix_out = Ring([Slot(ap=sb(f"mix_out{i}", [P, COLS]), sem=s_out[i]) for i in range(2)])
        squares = sb("squares", [P, C], mybir.dt.bfloat16)
        stats = sb("stats", [P, CT, NQ, 6])
        mean_var = sb("mean_var", [P, CT, 2])
        ln1 = sb("ln1", [P, CT, 3])
        powers = sb("powers", [P, 3, CT])
        qmax = sb("qmax", [P, 2, HEADS])
        qhalf = sb("qhalf", [P, HEADS, DIM_HEAD // 2])
        qsum = sb("qsum", [P, 2, 2, HEADS])
        kmax = sb("kmax", [P, 1 + NQ])
        ksum = sb("ksum", [P, NQ + 2])
        nrm = sb("nrm", [P, 2, 3, 2])
        ln2 = sb("ln2", [P, CT, 6])
        LT = NB * CT
        lg = sb("lg", [P, LOGITS, MAPS])
        sd_all = sb("sd_all", [P, LT])
        mean_all = sb("mean_all", [P, LT])
        skz_all = sb("skz", [P, TMAX, STREAMS, STREAMS])
        skp_all = sb("skp", [P, TMAX, STREAMS, STREAMS])
        skw_all = sb("skw", [P, TMAX, STREAMS, STREAMS])
        sku_all = sb("sku", [P, TMAX, STREAMS])
        skv_all = sb("skv", [P, TMAX, STREAMS])
        ska_all = sb("ska", [P, TMAX, STREAMS])
        skb_all = sb("skb", [P, TMAX, STREAMS])
        skr_all = sb("skr", [P, TMAX, STREAMS])
        pre_all = sb("pre", [P, TMAX, STREAMS])
        post_all = sb("post", [P, TMAX, STREAMS])
        soft_all = sb("soft", [P, TMAX, 2])

        big_t = stack.enter_context(nc.psum_tensor("big", [P, 4, BANK], F32))
        big = [Slot(ap=big_t[:, i, :]) for i in range(4)]
        tbank = Ring([Slot(ap=stack.enter_context(nc.psum_tensor(f"tbank{i}", [P, BANK], F32))) for i in range(2)])
        kc_bank = Slot(ap=stack.enter_context(nc.psum_tensor("kc_bank", [P, BANK], F32)))
        misc = Slot(ap=stack.enter_context(nc.psum_tensor("misc", [P, BANK], F32)))

        def f32(ap):
            return ap.bitcast(F32)

        def products(outp, left, right, after, sig, first=True, last=True):
            pairs = [(left[0], right[0]), (left[0], right[1]), (left[1], right[0])]
            token = None
            for i, (a, b) in enumerate(pairs):
                token = pe(after if i == 0 else (), sig if i == 2 else None,
                           nc.tensor.matmul, outp, a, b, start=(first and i == 0), stop=(last and i == 2))
            return token

        c0 = pool((), s_const, nc.gpsimd.memset, ident[:], 0.0)
        c_id = pool((c0,), s_const,
                    nc.gpsimd.affine_select, out=ident[:], in_=ident[:], compare_op=ALU.not_equal, fill=1.0, base=0, pattern=[[-1, P]], channel_multiplier=1)
        c1 = pool((), s_const, nc.gpsimd.memset, head_mask[:], 0.0)
        c1 = pool((c1,), s_const, nc.gpsimd.memset, head_mask[0:DIM_HEAD, 0:DIM_HEAD], SCALE)
        c_mask = pool((c1,), s_const, nc.gpsimd.memset, head_mask[DIM_HEAD:P, DIM_HEAD:P], SCALE)
        c2 = pool((), s_const, nc.gpsimd.memset, sel[:], 0.0)
        c2 = pool((c2,), s_const,
                  nc.gpsimd.affine_select, out=sel[:], in_=sel[:], compare_op=ALU.not_equal, fill=1.0, base=0, pattern=[[-1, MAPS]], channel_multiplier=1)
        c_sel = pool((c2,), s_const,
                     nc.gpsimd.affine_select, out=sel[:], in_=sel[:], compare_op=ALU.not_equal, fill=1.0, base=-MAPS, pattern=[[-1, MAPS]], channel_multiplier=1)
        c_w0 = pool((), s_const, nc.gpsimd.memset, f32(wmap[:]), 0.0)
        pool((), s_const, nc.gpsimd.memset, powers[:, 0, :], -0.5)
        c_pow = pool((), s_const, nc.gpsimd.memset, powers[:, 1, :], 0.5)

        small = [
            (bo_heads[:], bo.rearrange("(a c) -> a c", a=1).broadcast_to([P, C])),
            (base_rows[:], base.rearrange("(a m) -> a m", a=1).broadcast_to([P, MAPS])),
            (gcol[:], g),
            (gates[:, 0:1], gate.rearrange("(a c) -> a c", a=1).broadcast_to([P, 1])),
        ]
        landed = [sp((), s_small[i], nc.sync.dma_start, d, s) for i, (d, s) in enumerate(small)]
        c_bo = dve((landed[0],), s_stat, nc.vector.tensor_scalar, bo_heads[:], bo_heads[:], 1.0 / HEADS, None, ALU.mult)
        c_g = dve((landed[2],), s_stat, nc.vector.tensor_scalar, gcol[:], gcol[:], float(C) ** 0.5, None, ALU.mult)
        t = act((landed[3],), s_ska, nc.scalar.activation, gates[:, 1:2], gates[:, 0:1], ACT.Exp, scale=-1.0)
        t = dve((t,), s_stat, nc.vector.tensor_scalar, gates[:, 1:2], gates[:, 1:2], 1.0, None, ALU.add)
        t = dve((t,), s_stat, nc.vector.reciprocal, gates[:, 2:3], gates[:, 1:2])
        c_gate = dve((t,), s_stat, nc.vector.tensor_scalar, gates[:, 3:4], gates[:, 2:3], -1.0, 1.0, ALU.mult, ALU.add)

        def stage_load(src):
            slot = stage.take()
            width = 1
            for n in src.shape[1:]:
                width *= n
            ap = slot.ap[:, 0:width]
            if len(src.shape) == 3:
                ap = ap.rearrange("p (a b) -> p a b", a=src.shape[1])
            return slot, ap, sp(slot.free, slot.sem, nc.sync.dma_start, ap, src)

        def split_staged(staged, high, low, before=()):
            slot, ap, t = staged
            th = act((t, *before), s_split_h, nc.scalar.copy, high, ap)
            tl = pool((t, th, *before), s_split_l, nc.gpsimd.tensor_tensor, low, ap, f32(high), ALU.subtract)
            slot.release([tl])
            return th, tl

        def load_split(src, *args):
            return split_staged(stage_load(src), *args)

        w_ready = {}
        w_ready["k"] = load_split(wk_t.rearrange("(t p) o -> p t o", p=P), wk[0][:], wk[1][:])
        w_ready["v"] = load_split(wv_t.rearrange("(t p) o -> p t o", p=P), wv[0][:], wv[1][:])
        w_ready["o"] = load_split(wo_t.rearrange("(t p) o -> p t o", p=P), wo[0][:], wo[1][:])
        for j in range(2):
            w_ready["b"] = load_split(w_branch.rearrange("(t p) o -> p t o", p=P)[:, 2 * j:2 * j + 2, :],
                                      wb[0][:, 2 * j:2 * j + 2, :], wb[1][:, 2 * j:2 * j + 2, :])
        w_ready["m"] = load_split(w_maps_t.rearrange("(t p) o -> p t o", p=P),
                                  wmap_tiles[:, :, 0:MAPS], wmap_tiles[:, :, MAPS:2 * MAPS], (c_w0,))

        ctx_free = [[] for _ in range(NQ)]
        ctxt_free = [[] for _ in range(NQ)]
        ctx_ready = [None] * NQ
        ctxt_ready = [None] * NQ

        def load_context(b):
            rows = ctx[b].rearrange("(t p) n -> p t n", p=P)
            cols_t = ctx_t[b].rearrange("(t p) c -> p t c", p=P)
            parts = []
            for i in range(NQ):
                cols = slice(i * BANK, (i + 1) * BANK)
                parts.append((ctx_ready, ctx_free, i, rows[:, :, cols], [c[:, :, cols] for c in ctx_hl]))
            for i in range(NQ):
                nts = slice(i * NT // NQ, (i + 1) * NT // NQ)
                parts.append((ctxt_ready, ctxt_free, i, cols_t[:, nts, :], [c[:, nts, :] for c in ctxt_hl]))
            staged = stage_load(parts[0][3])
            yield
            for number, (ready, free, i, _, halves_of) in enumerate(parts):
                following = stage_load(parts[number + 1][3]) if number + 1 < len(parts) else None
                slot, ap, landed_t = staged
                tokens = []
                for k in range(2):
                    n = ap.shape[1] // 2
                    piece = slice(k * n, (k + 1) * n)
                    tokens += split_staged((slot, ap[:, piece, :], landed_t), *[h[:, piece, :] for h in halves_of], free[i])
                    yield
                ready[i] = tokens
                staged = following

        def transposed(sources, after):
            bank = tbank.take()
            for j, s in enumerate(sources):
                t = pe((*bank.free, *after, c_id) if j == 0 else (), s_tr if j == len(sources) - 1 else None,
                       nc.tensor.transpose, bank.ap[:, j * P:(j + 1) * P], s, ident[:])
            return bank, t

        def split_high(bank, written, slot, width):
            return act((written, *slot.free), s_th, nc.scalar.copy, slot.h[:, 0:width], bank.ap[:, 0:width])

        def split_low(bank, high, slot, width):
            t = dve((high, *slot.free), s_tl, nc.vector.tensor_tensor, slot.l[:, 0:width], bank.ap[:, 0:width],
                    f32(slot.h[:, 0:width]), ALU.subtract)
            bank.release([t])
            return t

        def split_bank(bank, written, slot, width):
            th = split_high(bank, written, slot, width)
            return th, split_low(bank, th, slot, width)

        urgent, steady = [], []
        pace = [0.0, 0.0]
        quiet, count, clock = [False], [0], [0]

        adv = [0]
        urgent_n = [0]

        def advance(queue):
            adv[0] += queue is steady
            urgent_n[0] += queue is urgent and len(queue) > 0
            while queue:
                if next(queue[0], queue) is queue:
                    queue.pop(0)
                else:
                    return

        def tick():
            if quiet[0]:
                return
            count[0] += 1
            clock[0] += 1
            pace[1] += pace[0]
            while pace[1] >= 1.0:
                pace[1] -= 1.0
                advance(steady)

        def pause(ticks):
            until = clock[0] + ticks
            while clock[0] < until:
                yield

        def work(weight=1):
            advance(urgent)
            tick()

        def left(queue):
            n = 0
            while queue:
                advance(queue)
                clock[0] += 1
                n += 1
                if queue is urgent:
                    advance(steady)
            return n

        def finish(queue):
            while queue:
                advance(queue)
                clock[0] += 1
                if queue is urgent:
                    advance(steady)

        m_free = []
        m_ready = []
        kexp_free = [[] for _ in range(NQ)]
        ksum_free = [[]]

        PER = NT // NQ

        def key_logits(dt, i):
            cols = slice(i * BANK, (i + 1) * BANK)
            for ct in range(CT):
                t = products(big[i].ap, [w[:, ct, dt * P:(dt + 1) * P] for w in wk], [c[:, ct, cols] for c in ctx_hl],
                             (*big[i].free, *ctx_ready[i], *w_ready["k"]), s_kmm, ct == 0, ct == CT - 1)
            ctx_free[i] = [t]
            return t

        def key_max(i, written):
            return dve((written, *ksum_free[0]), s_kmax, nc.vector.tensor_reduce, kmax[:, 1 + i:2 + i], big[i].ap, AX_X, ALU.max)

        def key_max_all(last):
            return dve((last, *ksum_free[0]), s_kmax, nc.vector.tensor_reduce, kmax[:, 0:1], kmax[:, 1:1 + NQ], AX_X, ALU.max, negate=True)

        def key_exp(i, maximum):
            t = act((maximum, *kexp_free[i], *ksum_free[0]), s_kexp, nc.scalar.activation,
                    k_exp[:, i * BANK:(i + 1) * BANK], big[i].ap, ACT.Exp, bias=kmax[:, 0:1], accum_out=ksum[:, i:i + 1])
            big[i].release([t])
            return t

        def key_sum(last_exp):
            t = dve((last_exp,), s_kmax, nc.vector.tensor_reduce, ksum[:, NQ:NQ + 1], ksum[:, 0:NQ], AX_X, ALU.add)
            return dve((t,), s_kmax, nc.vector.reciprocal, ksum[:, NQ + 1:NQ + 2], ksum[:, NQ:NQ + 1])

        def key_transpose(g, exp_done):
            bank, t = transposed([k_exp[:, (g * PER + j) * P:(g * PER + j + 1) * P] for j in range(PER)], (exp_done,))
            kexp_free[g] = [t]
            slot = split.take()
            return slot, bank, split_high(bank, t, slot, BANK)

        def key_low(slot, bank, high):
            return slot, (high, split_low(bank, high, slot, BANK))

        def key_context(g, slot, split_tokens):
            for j in range(PER):
                nt = g * PER + j
                t = products(kc_bank.ap[:, 0:C], [slot.h[:, j * P:(j + 1) * P], slot.l[:, j * P:(j + 1) * P]],
                             [c[:, nt, :] for c in ctxt_hl],
                             (*split_tokens, *ctxt_ready[g], *kc_bank.free), s_kc, nt == 0, nt == NT - 1)
            slot.release([t])
            ctxt_free[g] = [t]
            return t

        def output_matrix(dt, kc_done, rsum):
            t = dve((kc_done, rsum, *chain_raw.free), s_chd,
                    nc.vector.tensor_scalar, chain_raw.ap[:, 0:C], kc_bank.ap[:, 0:C], ksum[:, NQ + 1:NQ + 2], None, ALU.mult)
            kc_bank.release([t])
            ksum_free[0] = [t]
            yield
            bank, t = transposed([chain_raw.ap[:, j * P:(j + 1) * P] for j in range(CT)], (t,))
            chain_raw.release([t])
            split_tokens = split_bank(bank, t, chain_hl, CT * P)
            yield
            bank = tbank.take()
            for ct in range(CT):
                t = products(bank.ap[:, 0:P], [w[:, ct, dt * P:(dt + 1) * P] for w in wv],
                             [chain_hl.h[:, ct * P:(ct + 1) * P], chain_hl.l[:, ct * P:(ct + 1) * P]],
                             (*bank.free, *split_tokens, *w_ready["v"]), s_chain, ct == 0, ct == CT - 1)
            td = dve((t, c_mask, *chain_raw.free), s_chd,
                     nc.vector.tensor_tensor, chain_raw.ap[:, 0:P], bank.ap[:, 0:P], head_mask[:], ALU.mult)
            bank.release([td])
            th = act((td, t), s_cha, nc.scalar.copy, chain_hl.h[:, 0:P], chain_raw.ap[:, 0:P])
            tl = dve((th, t), s_chd,
                     nc.vector.tensor_tensor, chain_hl.l[:, 0:P], chain_raw.ap[:, 0:P], f32(chain_hl.h[:, 0:P]), ALU.subtract)
            yield
            bank = tbank.take()
            t = products(bank.ap[:, 0:C], [chain_hl.h[:, 0:P], chain_hl.l[:, 0:P]], [w[:, dt, :] for w in wo],
                         (*bank.free, th, tl, *w_ready["o"]), s_chain)
            chain_hl.release([t])
            td = dve((t, tl, c_bo), s_chd,
                     nc.vector.tensor_tensor, chain_raw.ap[:, 0:C], bank.ap[:, 0:C], bo_heads[:], ALU.add)
            bank.release([td])
            th = act((td, *m_free), s_cha, nc.scalar.copy, m_hl[0][:, dt, :], chain_raw.ap[:, 0:C])
            tl = dve((th, *m_free), s_chd,
                     nc.vector.tensor_tensor, m_hl[1][:, dt, :], chain_raw.ap[:, 0:C], f32(m_hl[0][:, dt, :]), ALU.subtract)
            chain_raw.release([tl])
            m_ready.append(th)
            m_ready.append(tl)

        def keys(b, early):
            m_ready.clear()
            exps = rsum = chain = None
            for dt in range(DT + 1):
                moved, tops = [], list(early) if dt == 0 else []
                for i in range(NQ):
                    if dt == DT:
                        if i == 0:
                            print("urgent left", left(urgent))
                            split_x(0)
                            split_x(1)
                        if i == 2:
                            query_logits(0)
                    elif i >= len(tops):
                        t = key_logits(dt, i)
                        if i and len(tops) < i:
                            tops.append(key_max(i - 1, before))
                        before = t
                    if chain:
                        next(chain, None)
                    work()
                    if exps and i >= 2:
                        moved.append(key_transpose(i - 2, exps[i - 2]))
                    work()
                    if exps and i >= 2:
                        moved[i - 2] = key_low(*moved[i - 2])
                if dt < DT:
                    while len(tops) < NQ:
                        tops.append(key_max(len(tops), before))
                    maximum = key_max_all(tops[-1])
                new = [None] * NQ
                if exps:
                    for g in range(NQ):
                        t = key_context(g, *moved[g])
                        if dt < DT:
                            new[g] = key_exp(g, maximum)
                        if g + 2 < NQ:
                            moved.append(key_transpose(g + 2, exps[g + 2]))
                            work()
                        work()
                        if g + 2 < NQ:
                            moved[g + 2] = key_low(*moved[g + 2])
                    chain = output_matrix(dt - 1, t, rsum)
                    next(chain)
                else:
                    for i in range(NQ):
                        new[i] = key_exp(i, maximum)
                        work()
                if dt < DT:
                    exps, rsum = new, key_sum(new[-1])
            return chain

        x_free = []

        def chunk_stats(i, after):
            for ct in range(CT):
                t = dve(after, s_stat, nc.vector.bn_stats, stats[:, ct, i, :], x_sb[:, ct, i * BANK:(i + 1) * BANK])
            return t

        def row_stats(t):
            for ct in range(CT):
                u = dve((t,), s_stat,
                        nc.vector.bn_aggr, mean_var[:, ct, :], stats[:, ct, :, :].rearrange("p a b -> p (a b)"))
            return u

        xq = {}

        def query_prepare(b):
            t = sp(x_free, s_x, nc.sync.dma_start, x_sb[:], x[b].rearrange("(t p) n -> p t n", p=P))
            xq["x"] = t
            yield
            yield
            for i in range(NQ):
                u = chunk_stats(i, (t,))
                yield
            u = row_stats(u)
            t = dve((u, *xq.get("ln1_free", ())), s_stat,
                    nc.vector.tensor_scalar, ln1[:, :, 0], mean_var[:, :, 1], LN_EPS, None, ALU.add)
            m = dve((u, *xq.get("ln1_free", ())), s_stat, nc.vector.tensor_scalar, ln1[:, :, 2], mean_var[:, :, 0], -1.0, None, ALU.mult)
            t = pool((t, c_pow), s_pow, nc.gpsimd.tensor_tensor, ln1[:, :, 1], ln1[:, :, 0], powers[:, 0, :], ALU.pow)
            yield
            for ct in range(CT):
                xq["centered", ct] = act((m,), s_xh, nc.scalar.activation, x_sb[:, ct, :], x_sb[:, ct, :],
                                         ACT.Identity, bias=ln1[:, ct, 2:3])
            yield
            tokens = []
            raw = stage.take()
            wq_raw = raw.ap.rearrange("p (t o) -> p t o", t=CT)
            c_wq = sp(raw.free, raw.sem, nc.sync.dma_start, wq_raw, wq_t.rearrange("(t p) o -> p t o", p=P))
            for ct in range(CT):
                th = act((t, c_wq, *xq.get("wq_free", ())), s_wqh,
                         nc.scalar.activation, wq[0][:, ct, :], wq_raw[:, ct, :], ACT.Copy, scale=ln1[:, ct, 1:2])
                tl = dve((th,), s_wq,
                         nc.vector.scalar_tensor_tensor, out=wq[1][:, ct, :], in0=wq_raw[:, ct, :], scalar=ln1[:, ct, 1:2], in1=f32(wq[0][:, ct, :]), op0=ALU.mult, op1=ALU.subtract)
                tokens += [th, tl]
            raw.release([tl])
            xq["wq"] = tokens

        def split_x(pair):
            slot = xc.take()
            cols = slice(pair * 2 * P, (pair + 1) * 2 * P)
            th = act((xq["centered", 0], xq["centered", 1], *slot.free), s_xh, nc.scalar.copy, slot.h[:], x_sb[:, :, cols])
            tl = pool((th, *slot.free), s_xl, nc.gpsimd.tensor_tensor, slot.l[:], x_sb[:, :, cols], f32(slot.h[:]), ALU.subtract)
            xq[pair] = (slot, (th, tl))

        qt = {}

        def query_logits(i):
            slot, tokens = xq[i // 2][:2]
            cols = slice((i % 2) * P, (i % 2 + 1) * P)
            bank = big[i % 2]
            for ct in range(CT):
                t = products(bank.ap, [slot.h[:, ct, cols], slot.l[:, ct, cols]], [w[:, ct, :] for w in wq],
                             (*bank.free, *tokens, *xq["wq"]), s_qmm, ct == 0, ct == CT - 1)
            if i % 2:
                slot.release([t])
            xq["wq_free"] = xq["ln1_free"] = [t]
            qt[i] = t

        heads = "p (h d) -> p h d"

        def query_max(i):
            qt["max", i] = dve((qt[i],), s_qmax, nc.vector.tensor_reduce, qmax[:, i % 2, :],
                               big[i % 2].ap.rearrange(heads, d=DIM_HEAD), AX_X, ALU.max)

        def query_exp(i):
            bank, buf, k = big[i % 2], q_sb.take(), i % 2
            exps = buf.ap[:].rearrange(heads, d=DIM_HEAD)
            t = dve((qt["max", i], *buf.free), s_qmax, nc.vector.tensor_tensor, exps, bank.ap.rearrange(heads, d=DIM_HEAD),
                    qmax[:, k, :].unsqueeze(2).broadcast_to([P, HEADS, DIM_HEAD]), ALU.subtract)
            bank.release([t])
            t = act((t,), s_qexp, nc.scalar.activation, buf.ap[:], buf.ap[:], ACT.Exp)
            qt[i] = (buf, t)

        def query_half(i):
            buf, t = qt[i]
            exps = buf.ap[:].rearrange(heads, d=DIM_HEAD)
            qt[i] = (buf, pool((t, qt.get("half_free")), s_qhalf, nc.gpsimd.tensor_tensor, qhalf[:], exps[:, :, 0:DIM_HEAD // 2],
                               exps[:, :, DIM_HEAD // 2:DIM_HEAD], ALU.add))

        def query_sum(i):
            k = i % 2
            qt["half_free"] = dve((qt[i][1],), s_qmax, nc.vector.tensor_reduce, qsum[:, k, 0, :], qhalf[:], AX_X, ALU.add)
            tick()
            qt["rsum", i] = dve((qt["half_free"], *qt.get(("rfree", k), ())), s_qmax, nc.vector.reciprocal, qsum[:, k, 1, :], qsum[:, k, 0, :])

        def query_normalise(i):
            buf, k = qt[i][0], i % 2
            exps = buf.ap[:].rearrange(heads, d=DIM_HEAD)
            t = pool((qt["rsum", i],), s_qn, nc.gpsimd.tensor_tensor, exps, exps,
                     qsum[:, k, 1, :].unsqueeze(2).broadcast_to([P, HEADS, DIM_HEAD]), ALU.mult)
            qt["rfree", k] = [t]
            qt[i] = (buf, t)

        def query_transpose(i):
            buf, t = qt[i]
            bank, t = transposed([buf.ap[:, j * P:(j + 1) * P] for j in range(DT)], (t,))
            buf.release([t])
            slot = split.take()
            qt[i] = (slot, bank, t)

        def query_high(i):
            slot, bank, t = qt[i]
            qt[i] = (slot, bank, split_high(bank, t, slot, HID))

        def query_low(i):
            slot, bank, th = qt[i]
            qt[i] = (slot, (th, split_low(bank, th, slot, HID)))

        def attention_out(i):
            slot, tokens = qt[i]
            bank = big[2 + (i // 2) % 2]
            half = slice((i % 2) * C, (i % 2 + 1) * C)
            for dt in range(DT):
                t = products(bank.ap[:, half], [slot.h[:, dt * P:(dt + 1) * P], slot.l[:, dt * P:(dt + 1) * P]],
                             [m[:, dt, :] for m in m_hl], ((*bank.free,) if i % 2 == 0 else ()) + (*tokens, *m_ready), s_o, dt == 0, dt == DT - 1)
            slot.release([t])
            m_free[:] = [t]
            qt[i] = t

        def square_pair(p):
            bank, k = big[2 + p % 2], p % 2
            t = None
            for j in range(2):
                t = act((qt[2 * p + 1], *qt.get(("nfree", k), ()), qt.get("sq")), s_ss,
                        nc.scalar.activation, squares[:], bank.ap[:, j * C:(j + 1) * C], ACT.Square, accum_out=nrm[:, k, 0, j:j + 1])
                qt["sq"] = t
            qt["norm", p] = pool((t, c_pow), s_pow, nc.gpsimd.tensor_tensor, nrm[:, k, 1, :], nrm[:, k, 0, :], powers[:, 1, 0:2], ALU.pow)

        def norm_pair(p):
            k = p % 2
            t = dve((qt["norm", p],), s_nrm, nc.vector.tensor_scalar, nrm[:, k, 1, :], nrm[:, k, 1, :], NORM_FLOOR, None, ALU.max)
            tick()
            qt["norm", p] = dve((t,), s_nrm, nc.vector.reciprocal, nrm[:, k, 2, :], nrm[:, k, 1, :])

        def scale_pair(p):
            bank, k = big[2 + p % 2], p % 2
            for j in range(2):
                buf = on.take()
                t = act((qt["norm", p], *buf.free), s_on,
                        nc.scalar.activation, buf.ap[:], bank.ap[:, j * C:(j + 1) * C], ACT.Copy, scale=nrm[:, k, 2, j:j + 1])
                qt["scaled", p, j] = (buf, t)
            bank.release([t])
            qt["nfree", k] = [t]

        def return_pair(p):
            for j in range(2):
                buf, t = qt["scaled", p, j]
                for ct in range(CT):
                    off = ct * 2 * P + j * P
                    u = pe((t, *kc_bank.free), s_ot,
                           nc.tensor.transpose, kc_bank.ap[:, off:off + P], buf.ap[:, ct * P:(ct + 1) * P], ident[:])
                buf.release([u])
            qt["returned", p] = u

        def residual_pair(p):
            for ct in range(CT):
                cols = slice(p * 2 * P, (p + 1) * 2 * P)
                v = dve((qt["returned", p], c_g, *xq[p][1]), s_x2, nc.vector.scalar_tensor_tensor, out=x_sb[:, ct, cols],
                        in0=kc_bank.ap[:, ct * 2 * P:(ct + 1) * 2 * P], scalar=gcol[:, ct:ct + 1],
                        in1=x_sb[:, ct, cols], op0=ALU.mult, op1=ALU.add)
                tick()
            kc_bank.release([v])
            xq["x2"] = v
            if p % 2:
                xq["stats"] = chunk_stats(p // 2, (*([xq["mv_free"]] if xq.get("mv_free") else []), v))

        LAG_T, LAG_O, LAG_N, LAG_S, LAG_R = 1, 2, 3, 4, 5

        def query_step(i, chain=None):
            def stage(lag, limit=NT):
                return 0 <= i - lag < limit

            def pair(lag):
                return (i - lag) // 2 if stage(lag) and (i - lag) % 2 else None

            if i + 1 < NT:
                query_logits(i + 1)
            if pair(LAG_R) is not None:
                return_pair(pair(LAG_R))
            if stage(0):
                query_max(i)
            tick()
            if stage(LAG_O):
                query_high(i - LAG_O)
                query_low(i - LAG_O)
            if chain:
                next(chain, None)
            if pair(LAG_S) is not None:
                norm_pair(pair(LAG_S))
                scale_pair(pair(LAG_S))
            if stage(LAG_T):
                query_sum(i - LAG_T)
                query_normalise(i - LAG_T)
            if stage(0):
                query_exp(i)
                query_half(i)
            tick()
            if stage(LAG_O):
                attention_out(i - LAG_O)
            if i % 2 and (i + 3) // 2 < NT // 2:
                split_x((i + 3) // 2)
            work(3)
            if pair(LAG_N) is not None:
                square_pair(pair(LAG_N))
            if pair(LAG_R) is not None:
                residual_pair(pair(LAG_R))
            if stage(LAG_T):
                query_transpose(i - LAG_T)
            tick()
            tick()

        def queries(b, chain, more):
            tops = []
            early = (NT - 1, NT, NT + 1)
            for i in range(NT + LAG_R):
                quiet[0] = i > NT
                query_step(i, chain)
                if more and i in early:
                    tops.append(key_max(early.index(i), key_logits(0, early.index(i))))
                quiet[0] = False
                tick()
            return tops

        def normalise_rows(b):
            t = row_stats(xq["stats"])
            s = dve((t, *xq.get("ln2_free", ())), s_stat,
                    nc.vector.tensor_scalar, ln2[:, :, 0], mean_var[:, :, 1], LN_EPS, None, ALU.add)
            m = dve((t,), s_stat, nc.vector.tensor_tensor, mean_all[:, b * CT:(b + 1) * CT], mean_var[:, :, 0], ln1[:, :, 2], ALU.subtract)
            xq["ln1_free"] = [*xq["ln1_free"], m]
            r = pool((s, c_pow), s_pow, nc.gpsimd.tensor_tensor, ln2[:, :, 1], ln2[:, :, 0], powers[:, 0, :], ALU.pow)
            d = pool((s,), s_pow,
                     nc.gpsimd.tensor_tensor, sd_all[:, b * CT:(b + 1) * CT], ln2[:, :, 0], powers[:, 1, :], ALU.pow)
            u = dve((r,), s_stat,
                    nc.vector.scalar_tensor_tensor, out=ln2[:, :, 2], in0=mean_var[:, :, 0], scalar=-1.0, in1=ln2[:, :, 1], op0=ALU.mult, op1=ALU.mult)
            w = dve((r,), s_stat, nc.vector.tensor_tensor, ln2[:, :, 3], ln2[:, :, 1], ln2[:, :, 1], ALU.mult)
            w = dve((w,), s_stat, nc.vector.tensor_tensor, ln2[:, :, 4], ln2[:, :, 3], mean_var[:, :, 1], ALU.mult)
            w = dve((w,), s_stat, nc.vector.tensor_scalar, ln2[:, :, 3], ln2[:, :, 4], RMS_EPS, None, ALU.add)
            w = pool((w,), s_pow, nc.gpsimd.tensor_tensor, ln2[:, :, 5], ln2[:, :, 3], powers[:, 0, :], ALU.pow)
            yield
            lns = [None]

            def layer_norm(i):
                cols = slice(i * BANK, (i + 1) * BANK)
                for ct in range(CT):
                    lns[0] = act((u, xq["x2"]), s_ln, nc.scalar.activation, x_sb[:, ct, cols], x_sb[:, ct, cols],
                                 ACT.Identity, bias=ln2[:, ct, 2:3], scale=ln2[:, ct, 1:2])

            layer_norm(0)
            for _ in range(WAIT_LN):
                yield
            per = BANK // C
            while misc.taken:
                yield
            misc.take()

            def multiply(i, slot, tokens):
                for j in range(per):
                    nt = i * per + j
                    for h, half in enumerate((slot.h, slot.l)):
                        t = pe((*misc.free, *tokens, *w_ready["m"]), s_lg,
                               nc.tensor.matmul, misc.ap[:, 0:C], wmap[:, nt * 2 * MAPS:nt * 2 * MAPS + P], half[:, j * C:(j + 1) * C], start=(nt == 0 and h == 0), stop=(nt == NT - 1 and h == 1))
                slot.release([t])
                return t

            for i in range(NT // per):
                if i % 2 == 0 and i // 2 + 1 < NQ:
                    layer_norm(i // 2 + 1)
                if i // 2 + 1 == NQ and i % 2 == 0:
                    spilled = sp(lns, s_spill, nc.sync.dma_start, ln_spill[b].rearrange("(t p) n -> p t n", p=P), x_sb[:])
                while not split_bg.ready():
                    yield
                slot = split_bg.take()
                bank, t = transposed([x_sb[:, ct, (i * per + j) * P:(i * per + j + 1) * P] for j in range(per) for ct in range(CT)], lns)
                xq["tr"] = t
                yield
                t = split_high(bank, t, slot, BANK)
                tick()
                tokens = t, split_low(bank, t, slot, BANK)
                yield
                yield
                done = multiply(i, slot, tokens)
            x_free[:] = [spilled, xq["tr"]]
            while not split_bg.ready():
                yield
            buf = on.take()
            map_sb = buf.ap[0:2 * MAPS, :]
            t = dve((done, *buf.free), s_lgd, nc.vector.tensor_copy, map_sb, misc.ap[0:2 * MAPS, 0:C])
            misc.release([t])
            bank = tbank.take()
            for ct in range(CT):
                u = pe((*bank.free, t, c_sel), s_lg,
                       nc.tensor.matmul, bank.ap[:, ct * MAPS:(ct + 1) * MAPS], map_sb[:, ct * P:(ct + 1) * P], sel[:], start=True, stop=True)
            buf.release([u])
            for ct in range(CT):
                v = dve((u, w, landed[1]), s_lgd,
                        nc.vector.scalar_tensor_tensor, out=lg[:, (b * CT + ct) % LOGITS, :], in0=bank.ap[:, ct * MAPS:(ct + 1) * MAPS], scalar=ln2[:, ct, 5:6], in1=base_rows[:], op0=ALU.mult, op1=ALU.add)
            bank.release([v])
            xq["ln2_free"] = [v, lns[-1]]
            xq["lg", b] = v
            xq["spilled", b] = [spilled, d, m]

        sk = {"free": []}

        def sinkhorn(batches):
            T = len(batches) * CT
            at = batches[0] * CT
            tiles = slice(at % LOGITS, at % LOGITS + T)
            lgs = [xq["lg", b] for b in batches]
            skz, skp, skw, sku, skv, ska, skb, skr, pre, post, soft = (
                a[:, 0:T] for a in (skz_all, skp_all, skw_all, sku_all, skv_all, ska_all, skb_all, skr_all,
                                    pre_all, post_all, soft_all))

            def over_j(v):
                return v[:].unsqueeze(2).broadcast_to([P, T, STREAMS, STREAMS])

            def over_i(v):
                return v[:].unsqueeze(3).broadcast_to([P, T, STREAMS, STREAMS])

            def by_column(m):
                return m[:].rearrange("p t i j -> p t j i")

            def D(after, method, *args, **kwargs):
                return dve(after, s_skd, method, *args, **kwargs)

            def A(after, method, *args, **kwargs):
                return act(after, s_ska, method, *args, **kwargs)

            t = D([*lgs, *sk["free"]],
                  nc.vector.tensor_scalar, skz[:].rearrange("p t i j -> p t (i j)"), lg[:, tiles, 0:RES], 1.0 / SINKHORN_TAU, None, ALU.mult)
            yield

            def negative_lse(target, m, spread, t, first):
                t = D([t], nc.vector.tensor_reduce, skr[:], m, AX_X, ALU.max)
                yield
                t = D([t], nc.vector.tensor_tensor, skp[:], skw[:] if not first else skz[:], spread(skr), ALU.subtract)
                yield
                t = A([t], nc.scalar.activation, skp[:], skp[:], ACT.Exp)
                yield
                t = D([t], nc.vector.tensor_reduce, ska[:], skp[:] if spread is over_i else by_column(skp), AX_X, ALU.add)
                yield
                t = A([t], nc.scalar.activation, ska[:], ska[:], ACT.Ln)
                yield
                return D([t],
                         nc.vector.scalar_tensor_tensor, out=target[:], in0=ska[:], scalar=-1.0, in1=skr[:], op0=ALU.mult, op1=ALU.subtract)

            t = yield from negative_lse(sku, skz[:], over_i, t, True)
            yield
            t = D([t], nc.vector.tensor_tensor, skw[:], skz[:], over_i(sku), ALU.add)
            yield
            t = yield from negative_lse(skv, by_column(skw), over_j, t, False)
            yield
            done = 1
            while True:
                t = D([t], nc.vector.tensor_tensor, skw[:], skz[:], over_i(sku), ALU.add)
                yield
                t = D([t], nc.vector.tensor_tensor, skw[:], skw[:], over_j(skv), ALU.add)
                yield
                t = A([t], nc.scalar.activation, skp[:], skw[:], ACT.Exp)
                yield
                if done == SINKHORN_ITERS:
                    break
                rounds = min(REFRESH, SINKHORN_ITERS - done)
                for r in range(rounds):
                    if r:
                        t = D([t], nc.vector.tensor_tensor, skw[:], skp[:], over_j(skb), ALU.mult)
                        yield
                    m = skw if r else skp
                    t = D([t], nc.vector.tensor_reduce, skr[:], m[:], AX_X, ALU.add)
                    yield
                    t = D([t], nc.vector.reciprocal, ska[:], skr[:])
                    yield
                    t = D([t], nc.vector.tensor_tensor, skw[:], skp[:], over_i(ska), ALU.mult)
                    yield
                    t = D([t], nc.vector.tensor_reduce, skr[:], by_column(skw), AX_X, ALU.add)
                    yield
                    t = D([t], nc.vector.reciprocal, skb[:], skr[:])
                    yield
                done += rounds
                for scaling, potential in ((ska, sku), (skb, skv)):
                    t = A([t], nc.scalar.activation, skr[:], scaling[:], ACT.Ln)
                    yield
                    t = D([t], nc.vector.tensor_tensor, potential[:], potential[:], skr[:], ALU.add)
                    yield
            t = D([t, c_gate], nc.vector.tensor_scalar, skp[:], skp[:], gates[:, 2:3], None, ALU.mult)
            yield
            diagonal = skp[:].rearrange("p t i j -> p t (i j)")[:, :, 0:RES:STREAMS + 1]
            t = D([t, *[tok for b in batches for tok in xq["spilled", b][1:]]],
                  nc.vector.scalar_tensor_tensor, out=diagonal, in0=diagonal, scalar=gates[:, 3:4], in1=sd_all[:, at:at + T].unsqueeze(2).broadcast_to([P, T, STREAMS]), op0=ALU.add, op1=ALU.add)
            yield
            for k, target in enumerate((pre, post)):
                cols = slice(RES + k * STREAMS, RES + (k + 1) * STREAMS)
                wide = [P, T, STREAMS]
                t = D([t], nc.vector.tensor_reduce, soft[:, :, 0], lg[:, tiles, cols], AX_X, ALU.max)
                yield
                t = D([t],
                      nc.vector.tensor_tensor, target[:], lg[:, tiles, cols], soft[:, :, 0].unsqueeze(2).broadcast_to(wide), ALU.subtract)
                yield
                t = A([t], nc.scalar.activation, target[:], target[:], ACT.Exp)
                yield
                t = D([t], nc.vector.tensor_reduce, soft[:, :, 0], target[:], AX_X, ALU.add)
                yield
                t = D([t], nc.vector.reciprocal, soft[:, :, 1], soft[:, :, 0])
                yield
                t = D([t],
                      nc.vector.tensor_tensor, target[:], target[:], soft[:, :, 1].unsqueeze(2).broadcast_to(wide), ALU.mult)
                yield
            sk["done"] = t
            yield

        def mix(batches):
            skp, pre, post = skp_all, pre_all, post_all
            buffers, loaded = mix_ln, []
            if batches[-1] == NB - 1:
                for ct in range(CT):
                    buffers.slots.append(Slot(ap=x_sb[:, ct, :], sem=s_mixld[1 + ct]))
                    buffers.slots[-1].free = list(x_free)

            def load_tile(tile):
                b, ct = batches[tile // CT], tile % CT
                slot = buffers.take()
                return slot, sp((xq["spilled", b][0], *slot.free), slot.sem,
                                nc.sync.dma_start, slot.ap, ln_spill[b, ct * P:(ct + 1) * P, :])

            for tile in range(len(batches) * CT):
                b, ct = batches[tile // CT], tile % CT
                tok = batches[0] * CT + tile
                slot_ln, t = loaded.pop(0) if loaded else load_tile(tile)
                ln = slot_ln.ap
                if tile + 1 < len(batches) * CT and buffers.ready():
                    loaded.append(load_tile(tile + 1))
                stream = [ln[:, j * COLS:(j + 1) * COLS] for j in range(STREAMS)]
                yield from pause(10)
                buf = mix_out.take()
                u = act((t, sk["done"], *buf.free), s_xpa,
                        nc.scalar.activation, buf.ap[:], stream[0], ACT.Copy, scale=pre[:, tile, 0:1])
                for j in range(1, STREAMS):
                    yield
                    u = dve((u,), s_xp,
                            nc.vector.scalar_tensor_tensor, out=buf.ap[:], in0=stream[j], scalar=pre[:, tile, j:j + 1], in1=buf.ap[:], op0=ALU.mult, op1=ALU.add)
                yield
                yield from pause(3)
                while not split_bg.ready():
                    yield
                slot = split_bg.take()
                bank, u = transposed([buf.ap[:, j * P:(j + 1) * P] for j in range(KT)], (u,))
                buf.release([u])
                yield from pause(2)
                th = split_high(bank, u, slot, BANK)
                yield from pause(1)
                tokens = th, split_low(bank, th, slot, BANK)
                yield from pause(3)
                bank = tbank.take()
                for k in range(KT):
                    y = products(bank.ap[:, 0:COLS], [slot.h[:, k * P:(k + 1) * P], slot.l[:, k * P:(k + 1) * P]],
                                 [w[:, k, :] for w in wb], (*bank.free, *tokens, *w_ready["b"]), s_y, k == 0, k == KT - 1)
                yield from pause(3)
                y = act((y, *y_sb.free), s_ya, nc.scalar.copy, y_sb.ap[:], bank.ap[:, 0:COLS])
                slot.release([y])
                bank.release([y])
                yield
                for i in range(STREAMS):
                    o = mix_out.take()
                    v = act((t, *o.free, sk["done"]), s_ma,
                            nc.scalar.activation, o.ap[:], stream[0], ACT.Identity, bias=mean_all[:, tok:tok + 1], scale=skp[:, tile, i, 0:1])
                    yield
                    for j in range(1, STREAMS):
                        v = dve((v,), s_md,
                                nc.vector.scalar_tensor_tensor, out=o.ap[:], in0=stream[j], scalar=skp[:, tile, i, j:j + 1], in1=o.ap[:], op0=ALU.mult, op1=ALU.add)
                        yield
                    v = dve((v, y), s_md,
                            nc.vector.scalar_tensor_tensor, out=o.ap[:], in0=y_sb.ap[:], scalar=post[:, tile, i:i + 1], in1=o.ap[:], op0=ALU.mult, op1=ALU.add)
                    w = sp((v,), o.sem, nc.sync.dma_start, out[b, ct * P:(ct + 1) * P, i * COLS:(i + 1) * COLS], o.ap[:])
                    o.release([w])
                    yield
                y_sb.release([v])
                slot_ln.release([v])
                yield
            sk["free"] = [v]

        def context_of(b):
            for _ in load_context(b):
                pass

        def after_batch(b):
            yield from normalise_rows(b)
            if b + 1 < NB:
                yield from query_prepare(b + 1)

        def group_work(batches):
            yield from sinkhorn(batches)
            yield from mix(batches)

        nc.scalar.preload_act_table_set("natural_log_exp_and_others")
        context_of(0)
        for _ in query_prepare(0):
            pass
        WAIT_LN = 5
        TICKS = 220
        ends, at = {}, 0
        for size in GROUPS:
            at += size
            ends[at - 1] = list(range(at - size, at))
        written = []
        for b in range(NB):
            chain = keys(b, written)
            if b + 1 < NB:
                urgent.append(load_context(b + 1))
            written = queries(b, chain, b + 1 < NB)
            finish(urgent)
            urgent.append(after_batch(b))
            print("urgent", b, urgent_n[0]); urgent_n[0]=0; print("ticks", count[0], adv[0], len(steady)); count[0] = 0; adv[0] = 0
            if b in ends:
                print("left", left(steady))
                finish(urgent)
                steady.append(group_work(ends[b]))
                following = [n for n in ends if n > b]
                if following:
                    n = len(ends[b])
                    pace[0] = (370 + 31 * n * CT) / (TICKS * (following[0] - b) - 26 * n * CT)
        finish(urgent)
        finish(steady)
        for s in (*s_out, s_spill):
            sp.wait(s, s.value)

        block = stack.enter_context(nc.Block())

        @block.sync
        def _(e):
            sp.replay()

        @block.tensor
        def _(e):
            pe.replay()

        @block.vector
        def _(e):
            dve.replay()

        @block.scalar
        def _(e):
            act.replay()

        @block.gpsimd
        def _(e):
            pool.replay()


def kernel(x, ctx_4096, L0_xattn_Wq, L0_xattn_Wk, L0_xattn_Wv, L0_xattn_Wo, L0_xattn_bo, L0_xattn_g, L0_ffn_W_res,
           L0_ffn_W_pre, L0_ffn_W_post, L0_ffn_H_res_base, L0_ffn_H_pre_base, L0_ffn_H_post_base, L0_ffn_gate, L0_ffn_W_branch):
    import numpy as np
    import concourse.bacc as bacc
    from concourse.bass_utils import run_bass_kernel_spmd

    host = {
        "x": x,
        "ctx": ctx_4096,
        "ctx_t": np.swapaxes(ctx_4096, 1, 2),
        "wq_t": np.transpose(L0_xattn_Wq),
        "wk_t": np.transpose(L0_xattn_Wk),
        "wv_t": np.transpose(L0_xattn_Wv),
        "wo_t": np.transpose(L0_xattn_Wo),
        "bo": L0_xattn_bo,
        "g": np.transpose(np.reshape(L0_xattn_g, (-1, P))),
        "w_maps_t": np.transpose(np.concatenate([L0_ffn_W_res, L0_ffn_W_pre, L0_ffn_W_post], axis=0)),
        "base": np.concatenate([np.reshape(L0_ffn_H_res_base, (-1,)), L0_ffn_H_pre_base, L0_ffn_H_post_base]),
        "gate": L0_ffn_gate,
        "w_branch": L0_ffn_W_branch,
    }
    nc = bacc.Bacc("TRN2", target_bir_lowering=False, num_devices=1)
    arrays, aps = {}, []
    for name, a in host.items():
        a = np.ascontiguousarray(a)
        arrays[f"in_{name}"] = a
        aps.append(nc.dram_tensor(f"in_{name}", a.shape, mybir.dt.from_np(a.dtype), kind="ExternalInput").ap())
    shape = tuple(x.shape)
    aps.append(nc.dram_tensor("ln_spill", shape, F32, kind="Internal").ap())
    aps.append(nc.dram_tensor("out_0", shape, F32, kind="ExternalOutput").ap())
    xattn_ffn(nc, *aps)
    r = run_bass_kernel_spmd(nc, [arrays], core_ids=[0])
    return r.results[0]["out_0"]
```

```python
from contextlib import ExitStack

import concourse.bass as bass
from concourse import mybir

ALU = mybir.AluOpType
ACT = mybir.ActivationFunctionType
AX_X = mybir.AxisListType.X
F32 = mybir.dt.float32
F32R = mybir.dt.float32r

P = 128
BANK = 512
LN_EPS = 1e-5
NORM_FLOOR = 1e-12
STREAMS = 4
SINKHORN_ITERS = 50
SINKHORN_TAU = 0.1
RMS_EPS = 1.1920929e-07
DIM_HEAD = 64
REFRESH = 10


class Queue:

    def __init__(self, engine):
        self.engine, self.steps, self.waited = engine, [], {}

    def __call__(self, after, signal, method, *args, **kwargs):
        for token in after:
            if token is not None:
                self.wait(*token)
        if signal is None:
            self.steps.append(lambda: method(*args, **kwargs))
            return None
        signal.value += signal.step
        self.steps.append(lambda: method(*args, **kwargs).then_inc(signal.handle, signal.step))
        return signal, signal.value

    def wait(self, signal, value):
        if self.waited.get(signal, 0) < value:
            self.waited[signal] = value
            self.steps.append(lambda: self.engine.wait_ge(signal.handle, value))

    def replay(self):
        for step in self.steps:
            step()


class Signal:

    def __init__(self, handle, step=1):
        self.handle, self.step, self.value = handle, step, 0


class Slot:

    def __init__(self, ap=None, h=None, l=None, sem=None):
        self.free, self.taken = [], False
        self.ap, self.h, self.l, self.sem = ap, h, l, sem

    def take(self):
        assert not self.taken
        self.taken = True
        return self

    def release(self, readers):
        self.free, self.taken = list(readers), False


class Ring:
    def __init__(self, slots):
        self.slots, self.n = slots, 0

    def take(self):
        assert self.ready()
        while self.slots[self.n % len(self.slots)].taken:
            self.n += 1
        self.n += 1
        return self.slots[(self.n - 1) % len(self.slots)].take()

    def ready(self):
        return not all(slot.taken for slot in self.slots)


def xattn_ffn(nc, x, ctx, ctx_t, wq_t, wk_t, wv_t, wo_t, bo, g, w_maps_t, base, gate, w_branch, ln_spill, out):
    NB, C, N = x.shape
    HID = wq_t.shape[1]
    CT = C // P
    NT = N // P
    DT = HID // P
    HEADS = HID // DIM_HEAD
    NQ = N // BANK
    COLS = N // STREAMS
    KT = COLS // P
    MAPS = w_maps_t.shape[1]
    RES = STREAMS * STREAMS
    GROUPS = [4, 4, 4, 4]
    TMAX = max(GROUPS) * CT
    LOGITS = 2 * TMAX
    SCALE = DIM_HEAD ** -0.5

    def logits_of(b, group=0):
        for size in GROUPS:
            if b < size:
                return (group % 2) * TMAX + b * CT
            b, group = b - size, group + 1

    stack = ExitStack()
    with stack:
        def sb(name, shape, dt=F32):
            return stack.enter_context(nc.sbuf_tensor(name, shape, dt))

        def signal(name, step=1):
            return Signal(stack.enter_context(nc.semaphore(name)), step)

        pe, dve, act = Queue(nc.tensor), Queue(nc.vector), Queue(nc.scalar)
        pool, sp = Queue(nc.gpsimd), Queue(nc.sync)

        s_const = signal("s_const")
        s_stage = [signal(f"s_stage{i}", 16) for i in range(2)]
        s_small = [signal(f"s_small{i}", 16) for i in range(4)]
        s_x = signal("s_x", 16)
        s_spill = signal("s_spill", 16)
        s_mixld = [signal(f"s_mixld{i}", 16) for i in range(1 + x.shape[1] // P)]
        s_out = [signal(f"s_out{i}", 16) for i in range(2)]
        s_split_h = signal("s_split_h")
        s_split_l = signal("s_split_l")
        s_stat = signal("s_stat")
        s_pow = signal("s_pow")
        s_wq = signal("s_wq")
        s_wqh = signal("s_wqh")
        s_xh = signal("s_xh")
        s_xl = signal("s_xl")
        s_kmm = signal("s_kmm")
        s_kmax = signal("s_kmax")
        s_kexp = signal("s_kexp")
        s_tr = signal("s_tr")
        s_th = signal("s_th")
        s_tl = signal("s_tl")
        s_kc = signal("s_kc")
        s_chain = signal("s_chain")
        s_chd = signal("s_chd")
        s_cha = signal("s_cha")
        s_qmm = signal("s_qmm")
        s_qmax = signal("s_qmax")
        s_qhalf = signal("s_qhalf")
        s_qexp = signal("s_qexp")
        s_qn = signal("s_qn")
        s_o = signal("s_o")
        s_ss = signal("s_ss")
        s_nrm = signal("s_nrm")
        s_on = signal("s_on")
        s_ot = signal("s_ot")
        s_x2 = signal("s_x2")
        s_ln = signal("s_ln")
        s_lg = signal("s_lg")
        s_lgd = signal("s_lgd")
        s_skd = signal("s_skd")
        s_ska = signal("s_ska")
        s_xp = signal("s_xp")
        s_xpa = signal("s_xpa")
        s_y = signal("s_y")
        s_ya = signal("s_ya")
        s_ma = signal("s_ma")
        s_md = signal("s_md")

        wk = [sb(f"wk_{h}", [P, CT, HID], F32R) for h in "hl"]
        wv = [sb(f"wv_{h}", [P, CT, HID], F32R) for h in "hl"]
        wo = [sb(f"wo_{h}", [P, DT, C], F32R) for h in "hl"]
        wb = [sb(f"wb_{h}", [P, KT, COLS], F32R) for h in "hl"]
        wmap = sb("wmap", [P, NT * 2 * MAPS + P], F32R)
        wmap_tiles = wmap[:, 0:NT * 2 * MAPS].rearrange("p (t m) -> p t m", t=NT)
        wq = [sb(f"wq_{h}", [P, CT, HID], F32R) for h in "hl"]
        ident = sb("ident", [P, P])
        head_mask = sb("head_mask", [P, P])
        sel = sb("sel", [2 * MAPS, MAPS])
        bo_heads = sb("bo_heads", [P, C])
        base_rows = sb("base_rows", [P, MAPS])
        gcol = sb("gcol", [P, CT])
        gates = sb("gates", [P, 4])
        x_sb = sb("x_sb", [P, CT, N])
        ctx_hl = [sb(f"ctx_{h}", [P, CT, N], F32R) for h in "hl"]
        ctxt_hl = [sb(f"ctxt_{h}", [P, NT, C], F32R) for h in "hl"]
        k_exp = sb("k_exp", [P, N])
        stage = Ring([Slot(ap=sb(f"stage{i}", [P, 1024]), sem=s_stage[i]) for i in range(2)])
        halves = [Slot(h=sb(f"split{i}_h", [P, BANK], F32R), l=sb(f"split{i}_l", [P, BANK], F32R)) for i in range(3)]
        split, split_bg = Ring(halves[:2]), Ring(halves[2:])
        chain_hl = Slot(h=sb("chain_h", [P, 2 * P], F32R), l=sb("chain_l", [P, 2 * P], F32R))
        chain_raw = Slot(ap=sb("chain_raw", [P, C]))
        m_hl = [sb(f"m_{h}", [P, DT, C], F32R) for h in "hl"]
        q_sb = Ring([Slot(ap=sb(f"q_sb{i}", [P, HID])) for i in range(2)])
        xc = Ring([Slot(h=sb(f"xc{i}_h", [P, CT, 2 * P], F32R), l=sb(f"xc{i}_l", [P, CT, 2 * P],
            F32R)) for i in range(2)])
        on = Ring([Slot(ap=sb(f"on{i}", [P, C])) for i in range(2)])
        y_sb = Slot(ap=sb("y_sb", [P, COLS]))
        mix_ln = Ring([Slot(ap=sb("mix_ln", [P, N])[:], sem=s_mixld[0])])
        mix_out = Ring([Slot(ap=sb(f"mix_out{i}", [P, COLS]), sem=s_out[i]) for i in range(2)])
        squares = sb("squares", [P, C], mybir.dt.bfloat16)
        stats = sb("stats", [P, CT, NQ, 6])
        mean_var = sb("mean_var", [P, CT, 2])
        ln1 = sb("ln1", [P, CT, 3])
        powers = sb("powers", [P, 3, CT])
        qmax = sb("qmax", [P, 2, HEADS])
        qhalf = sb("qhalf", [P, HEADS, DIM_HEAD // 2])
        qsum = sb("qsum", [P, 2, 2, HEADS])
        kmax = sb("kmax", [P, 1 + NQ])
        ksum = sb("ksum", [P, NQ + 2])
        nrm = sb("nrm", [P, 2, 3, 2])
        ln2 = sb("ln2", [P, CT, 6])
        LT = NB * CT
        lg = sb("lg", [P, LOGITS, MAPS])
        sd_all = sb("sd_all", [P, LT])
        mean_all = sb("mean_all", [P, LT])
        skz_all = sb("skz", [P, TMAX, STREAMS, STREAMS])
        skp_all = sb("skp", [P, TMAX, STREAMS, STREAMS])
        skw_all = sb("skw", [P, TMAX, STREAMS, STREAMS])
        sku_all = sb("sku", [P, TMAX, STREAMS])
        skv_all = sb("skv", [P, TMAX, STREAMS])
        ska_all = sb("ska", [P, TMAX, STREAMS])
        skb_all = sb("skb", [P, TMAX, STREAMS])
        skr_all = sb("skr", [P, TMAX, STREAMS])
        pre_all = sb("pre", [P, TMAX, STREAMS])
        post_all = sb("post", [P, TMAX, STREAMS])
        soft_all = sb("soft", [P, TMAX, 2])

        big_t = stack.enter_context(nc.psum_tensor("big", [P, 4, BANK], F32))
        big = [Slot(ap=big_t[:, i, :]) for i in range(4)]
        tbank = Ring([Slot(ap=stack.enter_context(nc.psum_tensor(f"tbank{i}", [P, BANK], F32))) for i in range(2)])
        kc_bank = Slot(ap=stack.enter_context(nc.psum_tensor("kc_bank", [P, BANK], F32)))
        misc = Slot(ap=stack.enter_context(nc.psum_tensor("misc", [P, BANK], F32)))

        def f32(ap):
            return ap.bitcast(F32)

        def products(outp, left, right, after, sig, first=True, last=True):
            pairs = [(left[0], right[0]), (left[0], right[1]), (left[1], right[0])]
            token = None
            for i, (a, b) in enumerate(pairs):
                token = pe(after if i == 0 else (), sig if i == 2 else None,
                           nc.tensor.matmul, outp, a, b, start=(first and i == 0), stop=(last and i == 2))
            return token

        c0 = pool((), s_const, nc.gpsimd.memset, ident[:], 0.0)
        c_id = pool((c0,), s_const,
                    nc.gpsimd.affine_select, out=ident[:], in_=ident[:], compare_op=ALU.not_equal, fill=1.0,
                    base=0, pattern=[[-1, P]], channel_multiplier=1)
        c1 = pool((), s_const, nc.gpsimd.memset, head_mask[:], 0.0)
        c1 = pool((c1,), s_const, nc.gpsimd.memset, head_mask[0:DIM_HEAD, 0:DIM_HEAD], SCALE)
        c_mask = pool((c1,), s_const, nc.gpsimd.memset, head_mask[DIM_HEAD:P, DIM_HEAD:P], SCALE)
        c2 = pool((), s_const, nc.gpsimd.memset, sel[:], 0.0)
        c2 = pool((c2,), s_const,
                  nc.gpsimd.affine_select, out=sel[:], in_=sel[:], compare_op=ALU.not_equal, fill=1.0, base=0,
                  pattern=[[-1, MAPS]], channel_multiplier=1)
        c_sel = pool((c2,), s_const,
                     nc.gpsimd.affine_select, out=sel[:], in_=sel[:], compare_op=ALU.not_equal, fill=1.0,
                     base=-MAPS, pattern=[[-1, MAPS]], channel_multiplier=1)
        c_w0 = pool((), s_const, nc.gpsimd.memset, f32(wmap[:]), 0.0)
        pool((), s_const, nc.gpsimd.memset, powers[:, 0, :], -0.5)
        c_pow = pool((), s_const, nc.gpsimd.memset, powers[:, 1, :], 0.5)

        small = [
            (bo_heads[:], bo.rearrange("(a c) -> a c", a=1).broadcast_to([P, C])),
            (base_rows[:], base.rearrange("(a m) -> a m", a=1).broadcast_to([P, MAPS])),
            (gcol[:], g),
            (gates[:, 0:1], gate.rearrange("(a c) -> a c", a=1).broadcast_to([P, 1])),
        ]
        landed = [sp((), s_small[i], nc.sync.dma_start, d, s) for i, (d, s) in enumerate(small)]
        c_bo = dve((landed[0],), s_stat, nc.vector.tensor_scalar, bo_heads[:], bo_heads[:], 1.0 / HEADS, None,
            ALU.mult)
        c_g = dve((landed[2],), s_stat, nc.vector.tensor_scalar, gcol[:], gcol[:], float(C) ** 0.5, None, ALU.mult)
        t = act((landed[3],), s_ska, nc.scalar.activation, gates[:, 1:2], gates[:, 0:1], ACT.Exp, scale=-1.0)
        t = dve((t,), s_stat, nc.vector.tensor_scalar, gates[:, 1:2], gates[:, 1:2], 1.0, None, ALU.add)
        t = dve((t,), s_stat, nc.vector.reciprocal, gates[:, 2:3], gates[:, 1:2])
        c_gate = dve((t,), s_stat, nc.vector.tensor_scalar, gates[:, 3:4], gates[:, 2:3], -1.0, 1.0, ALU.mult,
            ALU.add)

        def stage_load(src):
            slot = stage.take()
            width = 1
            for n in src.shape[1:]:
                width *= n
            ap = slot.ap[:, 0:width]
            if len(src.shape) == 3:
                ap = ap.rearrange("p (a b) -> p a b", a=src.shape[1])
            return slot, ap, sp(slot.free, slot.sem, nc.sync.dma_start, ap, src)

        def split_staged(staged, high, low, before=()):
            slot, ap, t = staged
            th = act((t, *before), s_split_h, nc.scalar.copy, high, ap)
            tl = pool((t, th, *before), s_split_l, nc.gpsimd.tensor_tensor, low, ap, f32(high), ALU.subtract)
            slot.release([tl])
            return th, tl

        def load_split(src, *args):
            return split_staged(stage_load(src), *args)

        w_ready = {}
        w_ready["k"] = load_split(wk_t.rearrange("(t p) o -> p t o", p=P), wk[0][:], wk[1][:])
        w_ready["v"] = load_split(wv_t.rearrange("(t p) o -> p t o", p=P), wv[0][:], wv[1][:])
        w_ready["o"] = load_split(wo_t.rearrange("(t p) o -> p t o", p=P), wo[0][:], wo[1][:])
        for j in range(2):
            w_ready["b"] = load_split(w_branch.rearrange("(t p) o -> p t o", p=P)[:, 2 * j:2 * j + 2, :],
                                      wb[0][:, 2 * j:2 * j + 2, :], wb[1][:, 2 * j:2 * j + 2, :])
        w_ready["m"] = load_split(w_maps_t.rearrange("(t p) o -> p t o", p=P),
                                  wmap_tiles[:, :, 0:MAPS], wmap_tiles[:, :, MAPS:2 * MAPS], (c_w0,))

        ctx_free = [[] for _ in range(NQ)]
        ctxt_free = [[] for _ in range(NQ)]
        ctx_ready = [None] * NQ
        ctxt_ready = [None] * NQ

        def load_context(b):
            rows = ctx[b].rearrange("(t p) n -> p t n", p=P)
            cols_t = ctx_t[b].rearrange("(t p) c -> p t c", p=P)
            parts = []
            for i in range(NQ):
                cols = slice(i * BANK, (i + 1) * BANK)
                parts.append((ctx_ready, ctx_free, i, rows[:, :, cols], [c[:, :, cols] for c in ctx_hl]))
            for i in range(NQ):
                nts = slice(i * NT // NQ, (i + 1) * NT // NQ)
                parts.append((ctxt_ready, ctxt_free, i, cols_t[:, nts, :], [c[:, nts, :] for c in ctxt_hl]))
            staged = stage_load(parts[0][3])
            yield
            for number, (ready, free, i, _, halves_of) in enumerate(parts):
                following = stage_load(parts[number + 1][3]) if number + 1 < len(parts) else None
                slot, ap, landed_t = staged
                tokens = []
                for k in range(2):
                    n = ap.shape[1] // 2
                    piece = slice(k * n, (k + 1) * n)
                    tokens += split_staged((slot, ap[:, piece, :], landed_t), *[h[:, piece,
                        :] for h in halves_of], free[i])
                    yield
                ready[i] = tokens
                staged = following

        def transposed(sources, after):
            bank = tbank.take()
            for j, s in enumerate(sources):
                t = pe((*bank.free, *after, c_id) if j == 0 else (), s_tr if j == len(sources) - 1 else None,
                       nc.tensor.transpose, bank.ap[:, j * P:(j + 1) * P], s, ident[:])
            return bank, t

        def split_high(bank, written, slot, width):
            return act((written, *slot.free), s_th, nc.scalar.copy, slot.h[:, 0:width], bank.ap[:, 0:width])

        def split_low(bank, high, slot, width):
            t = dve((high, *slot.free), s_tl, nc.vector.tensor_tensor, slot.l[:, 0:width], bank.ap[:, 0:width],
                    f32(slot.h[:, 0:width]), ALU.subtract)
            bank.release([t])
            return t

        def split_bank(bank, written, slot, width):
            th = split_high(bank, written, slot, width)
            return th, split_low(bank, th, slot, width)

        urgent, steady = [], []
        pace = [0.0, 0.0]
        clock = [0]
        quiet = [False]

        def advance(queue):
            while queue:
                if next(queue[0], queue) is queue:
                    queue.pop(0)
                else:
                    return

        def tick():
            if quiet[0]:
                return
            clock[0] += 1
            pace[1] += pace[0]
            while pace[1] >= 1.0:
                pace[1] -= 1.0
                advance(steady)

        def pause(ticks):
            until = clock[0] + ticks
            while clock[0] < until:
                yield

        def work():
            advance(urgent)
            tick()

        def finish(queue):
            while queue:
                advance(queue)
                clock[0] += 1
                if queue is urgent:
                    advance(steady)

        m_free = []
        m_ready = []
        kexp_free = [[] for _ in range(NQ)]
        ksum_free = [[]]

        PER = NT // NQ

        def key_logits(dt, i):
            cols = slice(i * BANK, (i + 1) * BANK)
            for ct in range(CT):
                t = products(big[i].ap, [w[:, ct, dt * P:(dt + 1) * P] for w in wk], [c[:, ct, cols] for c in ctx_hl],
                             (*big[i].free, *ctx_ready[i], *w_ready["k"]), s_kmm, ct == 0, ct == CT - 1)
            ctx_free[i] = [t]
            return t

        def key_max(i, written):
            return dve((written, *ksum_free[0]), s_kmax, nc.vector.tensor_reduce, kmax[:, 1 + i:2 + i],
                big[i].ap, AX_X, ALU.max)

        def key_max_all(last):
            return dve((last, *ksum_free[0]), s_kmax, nc.vector.tensor_reduce, kmax[:, 0:1], kmax[:, 1:1 + NQ],
                AX_X, ALU.max, negate=True)

        def key_exp(i, maximum):
            t = act((maximum, *kexp_free[i], *ksum_free[0]), s_kexp, nc.scalar.activation,
                    k_exp[:, i * BANK:(i + 1) * BANK], big[i].ap, ACT.Exp, bias=kmax[:, 0:1], accum_out=ksum[:,
                        i:i + 1])
            big[i].release([t])
            return t

        def key_sum(last_exp):
            t = dve((last_exp,), s_kmax, nc.vector.tensor_reduce, ksum[:, NQ:NQ + 1], ksum[:, 0:NQ], AX_X, ALU.add)
            return dve((t,), s_kmax, nc.vector.reciprocal, ksum[:, NQ + 1:NQ + 2], ksum[:, NQ:NQ + 1])

        def key_transpose(g, exp_done):
            bank, t = transposed([k_exp[:, (g * PER + j) * P:(g * PER + j + 1) * P] for j in range(PER)], (exp_done,))
            kexp_free[g] = [t]
            slot = split.take()
            return slot, bank, split_high(bank, t, slot, BANK)

        def key_low(slot, bank, high):
            return slot, (high, split_low(bank, high, slot, BANK))

        def key_context(g, slot, split_tokens):
            for j in range(PER):
                nt = g * PER + j
                t = products(kc_bank.ap[:, 0:C], [slot.h[:, j * P:(j + 1) * P], slot.l[:, j * P:(j + 1) * P]],
                             [c[:, nt, :] for c in ctxt_hl],
                             (*split_tokens, *ctxt_ready[g], *kc_bank.free), s_kc, nt == 0, nt == NT - 1)
            slot.release([t])
            ctxt_free[g] = [t]
            return t

        def output_matrix(dt, kc_done, rsum):
            t = dve((kc_done, rsum, *chain_raw.free), s_chd,
                    nc.vector.tensor_scalar, chain_raw.ap[:, 0:C], kc_bank.ap[:, 0:C], ksum[:, NQ + 1:NQ + 2],
                    None, ALU.mult)
            kc_bank.release([t])
            ksum_free[0] = [t]
            yield
            bank, t = transposed([chain_raw.ap[:, j * P:(j + 1) * P] for j in range(CT)], (t,))
            chain_raw.release([t])
            split_tokens = split_bank(bank, t, chain_hl, CT * P)
            yield
            bank = tbank.take()
            for ct in range(CT):
                t = products(bank.ap[:, 0:P], [w[:, ct, dt * P:(dt + 1) * P] for w in wv],
                             [chain_hl.h[:, ct * P:(ct + 1) * P], chain_hl.l[:, ct * P:(ct + 1) * P]],
                             (*bank.free, *split_tokens, *w_ready["v"]), s_chain, ct == 0, ct == CT - 1)
            td = dve((t, c_mask, *chain_raw.free), s_chd,
                     nc.vector.tensor_tensor, chain_raw.ap[:, 0:P], bank.ap[:, 0:P], head_mask[:], ALU.mult)
            bank.release([td])
            th = act((td, t), s_cha, nc.scalar.copy, chain_hl.h[:, 0:P], chain_raw.ap[:, 0:P])
            tl = dve((th, t), s_chd,
                     nc.vector.tensor_tensor, chain_hl.l[:, 0:P], chain_raw.ap[:, 0:P], f32(chain_hl.h[:, 0:P]),
                     ALU.subtract)
            yield
            bank = tbank.take()
            t = products(bank.ap[:, 0:C], [chain_hl.h[:, 0:P], chain_hl.l[:, 0:P]], [w[:, dt, :] for w in wo],
                         (*bank.free, th, tl, *w_ready["o"]), s_chain)
            chain_hl.release([t])
            td = dve((t, tl, c_bo), s_chd,
                     nc.vector.tensor_tensor, chain_raw.ap[:, 0:C], bank.ap[:, 0:C], bo_heads[:], ALU.add)
            bank.release([td])
            th = act((td, *m_free), s_cha, nc.scalar.copy, m_hl[0][:, dt, :], chain_raw.ap[:, 0:C])
            tl = dve((th, *m_free), s_chd,
                     nc.vector.tensor_tensor, m_hl[1][:, dt, :], chain_raw.ap[:, 0:C], f32(m_hl[0][:, dt, :]),
                     ALU.subtract)
            chain_raw.release([tl])
            m_ready.append(th)
            m_ready.append(tl)

        def keys(b, early):
            m_ready.clear()
            exps = rsum = chain = None
            for dt in range(DT + 1):
                moved, tops = [], list(early) if dt == 0 else []
                for i in range(NQ):
                    if dt == DT:
                        if i == 0:
                            finish(urgent)
                            split_x(0)
                            split_x(1)
                        if i == 2:
                            query_logits(0)
                    elif i >= len(tops):
                        t = key_logits(dt, i)
                        if i and len(tops) < i:
                            tops.append(key_max(i - 1, before))
                        before = t
                    if chain:
                        next(chain, None)
                    work()
                    if exps and i >= 2:
                        moved.append(key_transpose(i - 2, exps[i - 2]))
                    work()
                    if exps and i >= 2:
                        moved[i - 2] = key_low(*moved[i - 2])
                if dt < DT:
                    while len(tops) < NQ:
                        tops.append(key_max(len(tops), before))
                    maximum = key_max_all(tops[-1])
                new = [None] * NQ
                if exps:
                    for g in range(NQ):
                        t = key_context(g, *moved[g])
                        if dt < DT:
                            new[g] = key_exp(g, maximum)
                        if g + 2 < NQ:
                            moved.append(key_transpose(g + 2, exps[g + 2]))
                            work()
                        work()
                        if g + 2 < NQ:
                            moved[g + 2] = key_low(*moved[g + 2])
                    chain = output_matrix(dt - 1, t, rsum)
                    next(chain)
                else:
                    for i in range(NQ):
                        new[i] = key_exp(i, maximum)
                        work()
                if dt < DT:
                    exps, rsum = new, key_sum(new[-1])
            return chain

        x_free = []

        def chunk_stats(i, after):
            for ct in range(CT):
                t = dve(after, s_stat, nc.vector.bn_stats, stats[:, ct, i, :], x_sb[:, ct, i * BANK:(i + 1) * BANK])
            return t

        def row_stats(t):
            for ct in range(CT):
                u = dve((t,), s_stat,
                        nc.vector.bn_aggr, mean_var[:, ct, :], stats[:, ct, :, :].rearrange("p a b -> p (a b)"))
            return u

        xq = {}

        def query_prepare(b):
            t = sp(x_free, s_x, nc.sync.dma_start, x_sb[:], x[b].rearrange("(t p) n -> p t n", p=P))
            xq["x"] = t
            yield
            yield
            for i in range(NQ):
                u = chunk_stats(i, (t,))
                yield
            u = row_stats(u)
            t = dve((u, *xq.get("ln1_free", ())), s_stat,
                    nc.vector.tensor_scalar, ln1[:, :, 0], mean_var[:, :, 1], LN_EPS, None, ALU.add)
            m = dve((u, *xq.get("ln1_free", ())), s_stat, nc.vector.tensor_scalar, ln1[:, :, 2], mean_var[:, :,
                0], -1.0, None, ALU.mult)
            t = pool((t, c_pow), s_pow, nc.gpsimd.tensor_tensor, ln1[:, :, 1], ln1[:, :, 0], powers[:, 0, :], ALU.pow)
            yield
            for ct in range(CT):
                xq["centered", ct] = act((m,), s_xh, nc.scalar.activation, x_sb[:, ct, :], x_sb[:, ct, :],
                                         ACT.Identity, bias=ln1[:, ct, 2:3])
            yield
            tokens = []
            raw = stage.take()
            wq_raw = raw.ap.rearrange("p (t o) -> p t o", t=CT)
            c_wq = sp(raw.free, raw.sem, nc.sync.dma_start, wq_raw, wq_t.rearrange("(t p) o -> p t o", p=P))
            for ct in range(CT):
                th = act((t, c_wq, *xq.get("wq_free", ())), s_wqh,
                         nc.scalar.activation, wq[0][:, ct, :], wq_raw[:, ct, :], ACT.Copy, scale=ln1[:, ct, 1:2])
                tl = dve((th,), s_wq,
                         nc.vector.scalar_tensor_tensor, out=wq[1][:, ct, :], in0=wq_raw[:, ct, :], scalar=ln1[:,
                         ct, 1:2], in1=f32(wq[0][:, ct, :]), op0=ALU.mult, op1=ALU.subtract)
                tokens += [th, tl]
            raw.release([tl])
            xq["wq"] = tokens

        def split_x(pair):
            slot = xc.take()
            cols = slice(pair * 2 * P, (pair + 1) * 2 * P)
            th = act((xq["centered", 0], xq["centered", 1], *slot.free), s_xh, nc.scalar.copy, slot.h[:], x_sb[:,
                :, cols])
            tl = pool((th, *slot.free), s_xl, nc.gpsimd.tensor_tensor, slot.l[:], x_sb[:, :, cols],
                f32(slot.h[:]), ALU.subtract)
            xq[pair] = (slot, (th, tl))

        qt = {}

        def query_logits(i):
            slot, tokens = xq[i // 2][:2]
            cols = slice((i % 2) * P, (i % 2 + 1) * P)
            bank = big[i % 2]
            for ct in range(CT):
                t = products(bank.ap, [slot.h[:, ct, cols], slot.l[:, ct, cols]], [w[:, ct, :] for w in wq],
                             (*bank.free, *tokens, *xq["wq"]), s_qmm, ct == 0, ct == CT - 1)
            if i % 2:
                slot.release([t])
            xq["wq_free"] = xq["ln1_free"] = [t]
            qt[i] = t

        heads = "p (h d) -> p h d"

        def query_max(i):
            qt["max", i] = dve((qt[i],), s_qmax, nc.vector.tensor_reduce, qmax[:, i % 2, :],
                               big[i % 2].ap.rearrange(heads, d=DIM_HEAD), AX_X, ALU.max)

        def query_exp(i):
            bank, buf, k = big[i % 2], q_sb.take(), i % 2
            exps = buf.ap[:].rearrange(heads, d=DIM_HEAD)
            t = dve((qt["max", i], *buf.free), s_qmax, nc.vector.tensor_tensor, exps, bank.ap.rearrange(heads,
                d=DIM_HEAD),
                    qmax[:, k, :].unsqueeze(2).broadcast_to([P, HEADS, DIM_HEAD]), ALU.subtract)
            bank.release([t])
            t = act((t,), s_qexp, nc.scalar.activation, buf.ap[:], buf.ap[:], ACT.Exp)
            qt[i] = (buf, t)

        def query_half(i):
            buf, t = qt[i]
            exps = buf.ap[:].rearrange(heads, d=DIM_HEAD)
            qt[i] = (buf, pool((t, qt.get("half_free")), s_qhalf, nc.gpsimd.tensor_tensor, qhalf[:], exps[:, :,
                0:DIM_HEAD // 2],
                               exps[:, :, DIM_HEAD // 2:DIM_HEAD], ALU.add))

        def query_sum(i):
            k = i % 2
            qt["half_free"] = dve((qt[i][1],), s_qmax, nc.vector.tensor_reduce, qsum[:, k, 0, :], qhalf[:], AX_X,
                ALU.add)
            tick()
            qt["rsum", i] = dve((qt["half_free"], *qt.get(("rfree", k), ())), s_qmax, nc.vector.reciprocal,
                qsum[:, k, 1, :], qsum[:, k, 0, :])

        def query_normalise(i):
            buf, k = qt[i][0], i % 2
            exps = buf.ap[:].rearrange(heads, d=DIM_HEAD)
            t = pool((qt["rsum", i],), s_qn, nc.gpsimd.tensor_tensor, exps, exps,
                     qsum[:, k, 1, :].unsqueeze(2).broadcast_to([P, HEADS, DIM_HEAD]), ALU.mult)
            qt["rfree", k] = [t]
            qt[i] = (buf, t)

        def query_transpose(i):
            buf, t = qt[i]
            bank, t = transposed([buf.ap[:, j * P:(j + 1) * P] for j in range(DT)], (t,))
            buf.release([t])
            slot = split.take()
            qt[i] = (slot, bank, t)

        def query_high(i):
            slot, bank, t = qt[i]
            qt[i] = (slot, bank, split_high(bank, t, slot, HID))

        def query_low(i):
            slot, bank, th = qt[i]
            qt[i] = (slot, (th, split_low(bank, th, slot, HID)))

        def attention_out(i):
            slot, tokens = qt[i]
            bank = big[2 + (i // 2) % 2]
            half = slice((i % 2) * C, (i % 2 + 1) * C)
            for dt in range(DT):
                t = products(bank.ap[:, half], [slot.h[:, dt * P:(dt + 1) * P], slot.l[:, dt * P:(dt + 1) * P]],
                             [m[:, dt, :] for m in m_hl], ((*bank.free,) if i % 2 == 0 else ()) + (*tokens,
                                 *m_ready), s_o, dt == 0, dt == DT - 1)
            slot.release([t])
            m_free[:] = [t]
            qt[i] = t

        def square_pair(p):
            bank, k = big[2 + p % 2], p % 2
            t = None
            for j in range(2):
                t = act((qt[2 * p + 1], *qt.get(("nfree", k), ()), qt.get("sq")), s_ss,
                        nc.scalar.activation, squares[:], bank.ap[:, j * C:(j + 1) * C], ACT.Square,
                        accum_out=nrm[:, k, 0, j:j + 1])
                qt["sq"] = t
            qt["norm", p] = pool((t, c_pow), s_pow, nc.gpsimd.tensor_tensor, nrm[:, k, 1, :], nrm[:, k, 0, :],
                powers[:, 1, 0:2], ALU.pow)

        def norm_pair(p):
            k = p % 2
            t = dve((qt["norm", p],), s_nrm, nc.vector.tensor_scalar, nrm[:, k, 1, :], nrm[:, k, 1, :],
                NORM_FLOOR, None, ALU.max)
            tick()
            qt["norm", p] = dve((t,), s_nrm, nc.vector.reciprocal, nrm[:, k, 2, :], nrm[:, k, 1, :])

        def scale_pair(p):
            bank, k = big[2 + p % 2], p % 2
            for j in range(2):
                buf = on.take()
                t = act((qt["norm", p], *buf.free), s_on,
                        nc.scalar.activation, buf.ap[:], bank.ap[:, j * C:(j + 1) * C], ACT.Copy, scale=nrm[:, k,
                        2, j:j + 1])
                qt["scaled", p, j] = (buf, t)
            bank.release([t])
            qt["nfree", k] = [t]

        def return_pair(p):
            for j in range(2):
                buf, t = qt["scaled", p, j]
                for ct in range(CT):
                    off = ct * 2 * P + j * P
                    u = pe((t, *kc_bank.free), s_ot,
                           nc.tensor.transpose, kc_bank.ap[:, off:off + P], buf.ap[:, ct * P:(ct + 1) * P], ident[:])
                buf.release([u])
            qt["returned", p] = u

        def residual_pair(p):
            for ct in range(CT):
                cols = slice(p * 2 * P, (p + 1) * 2 * P)
                v = dve((qt["returned", p], c_g, *xq[p][1]), s_x2, nc.vector.scalar_tensor_tensor, out=x_sb[:,
                    ct, cols],
                        in0=kc_bank.ap[:, ct * 2 * P:(ct + 1) * 2 * P], scalar=gcol[:, ct:ct + 1],
                        in1=x_sb[:, ct, cols], op0=ALU.mult, op1=ALU.add)
                tick()
            kc_bank.release([v])
            xq["x2"] = v
            if p % 2:
                xq["stats"] = chunk_stats(p // 2, (*([xq["mv_free"]] if xq.get("mv_free") else []), v))

        LAG_T, LAG_O, LAG_N, LAG_S, LAG_R = 1, 2, 3, 4, 5

        def query_step(i, chain=None):
            def stage(lag, limit=NT):
                return 0 <= i - lag < limit

            def pair(lag):
                return (i - lag) // 2 if stage(lag) and (i - lag) % 2 else None

            if i + 1 < NT:
                query_logits(i + 1)
            if pair(LAG_R) is not None:
                return_pair(pair(LAG_R))
            if stage(0):
                query_max(i)
            tick()
            if stage(LAG_O):
                query_high(i - LAG_O)
                query_low(i - LAG_O)
            if chain:
                next(chain, None)
            if pair(LAG_S) is not None:
                norm_pair(pair(LAG_S))
                scale_pair(pair(LAG_S))
            if stage(LAG_T):
                query_sum(i - LAG_T)
                query_normalise(i - LAG_T)
            if stage(0):
                query_exp(i)
                query_half(i)
            tick()
            if stage(LAG_O):
                attention_out(i - LAG_O)
            if i % 2 and (i + 3) // 2 < NT // 2:
                split_x((i + 3) // 2)
            work()
            if pair(LAG_N) is not None:
                square_pair(pair(LAG_N))
            if pair(LAG_R) is not None:
                residual_pair(pair(LAG_R))
            if stage(LAG_T):
                query_transpose(i - LAG_T)
            tick()
            tick()

        def queries(b, chain, more):
            tops = []
            early = (NT - 1, NT, NT + 1)
            for i in range(NT + LAG_R):
                quiet[0] = i > NT
                query_step(i, chain)
                if more and i in early:
                    tops.append(key_max(early.index(i), key_logits(0, early.index(i))))
                quiet[0] = False
                tick()
            return tops

        def normalise_rows(b):
            t = row_stats(xq["stats"])
            s = dve((t, *xq.get("ln2_free", ())), s_stat,
                    nc.vector.tensor_scalar, ln2[:, :, 0], mean_var[:, :, 1], LN_EPS, None, ALU.add)
            m = dve((t,), s_stat, nc.vector.tensor_tensor, mean_all[:, b * CT:(b + 1) * CT], mean_var[:, :, 0],
                ln1[:, :, 2], ALU.subtract)
            xq["ln1_free"] = [*xq["ln1_free"], m]
            r = pool((s, c_pow), s_pow, nc.gpsimd.tensor_tensor, ln2[:, :, 1], ln2[:, :, 0], powers[:, 0, :], ALU.pow)
            d = pool((s,), s_pow,
                     nc.gpsimd.tensor_tensor, sd_all[:, b * CT:(b + 1) * CT], ln2[:, :, 0], powers[:, 1, :], ALU.pow)
            u = dve((r,), s_stat,
                    nc.vector.scalar_tensor_tensor, out=ln2[:, :, 2], in0=mean_var[:, :, 0], scalar=-1.0,
                    in1=ln2[:, :, 1], op0=ALU.mult, op1=ALU.mult)
            w = dve((r,), s_stat, nc.vector.tensor_tensor, ln2[:, :, 3], ln2[:, :, 1], ln2[:, :, 1], ALU.mult)
            w = dve((w,), s_stat, nc.vector.tensor_tensor, ln2[:, :, 4], ln2[:, :, 3], mean_var[:, :, 1], ALU.mult)
            w = dve((w,), s_stat, nc.vector.tensor_scalar, ln2[:, :, 3], ln2[:, :, 4], RMS_EPS, None, ALU.add)
            w = pool((w,), s_pow, nc.gpsimd.tensor_tensor, ln2[:, :, 5], ln2[:, :, 3], powers[:, 0, :], ALU.pow)
            yield
            lns = [None]

            def layer_norm(i):
                cols = slice(i * BANK, (i + 1) * BANK)
                for ct in range(CT):
                    lns[0] = act((u, xq["x2"]), s_ln, nc.scalar.activation, x_sb[:, ct, cols], x_sb[:, ct, cols],
                                 ACT.Identity, bias=ln2[:, ct, 2:3], scale=ln2[:, ct, 1:2])

            layer_norm(0)
            for _ in range(5):
                yield
            per = BANK // C
            while misc.taken:
                yield
            misc.take()

            def multiply(i, slot, tokens):
                for j in range(per):
                    nt = i * per + j
                    for h, half in enumerate((slot.h, slot.l)):
                        t = pe((*misc.free, *tokens, *w_ready["m"]), s_lg,
                               nc.tensor.matmul, misc.ap[:, 0:C], wmap[:, nt * 2 * MAPS:nt * 2 * MAPS + P],
                               half[:, j * C:(j + 1) * C], start=(nt == 0 and h == 0), stop=(nt == NT - 1 and h == 1))
                slot.release([t])
                return t

            for i in range(NT // per):
                if i % 2 == 0 and i // 2 + 1 < NQ:
                    layer_norm(i // 2 + 1)
                if i // 2 + 1 == NQ and i % 2 == 0:
                    spilled = sp(lns, s_spill, nc.sync.dma_start, ln_spill[b].rearrange("(t p) n -> p t n", p=P),
                        x_sb[:])
                while not split_bg.ready():
                    yield
                slot = split_bg.take()
                bank, t = transposed([x_sb[:, ct,
                    (i * per + j) * P:(i * per + j + 1) * P] for j in range(per) for ct in range(CT)], lns)
                xq["tr"] = t
                yield
                t = split_high(bank, t, slot, BANK)
                tick()
                tokens = t, split_low(bank, t, slot, BANK)
                yield
                yield
                done = multiply(i, slot, tokens)
            x_free[:] = [spilled, xq["tr"]]
            while not split_bg.ready():
                yield
            buf = on.take()
            map_sb = buf.ap[0:2 * MAPS, :]
            t = dve((done, *buf.free), s_lgd, nc.vector.tensor_copy, map_sb, misc.ap[0:2 * MAPS, 0:C])
            misc.release([t])
            bank = tbank.take()
            for ct in range(CT):
                u = pe((*bank.free, t, c_sel), s_lg,
                       nc.tensor.matmul, bank.ap[:, ct * MAPS:(ct + 1) * MAPS], map_sb[:, ct * P:(ct + 1) * P],
                       sel[:], start=True, stop=True)
            buf.release([u])
            for ct in range(CT):
                v = dve((u, w, landed[1]), s_lgd,
                        nc.vector.scalar_tensor_tensor, out=lg[:, logits_of(b) + ct, :], in0=bank.ap[:,
                        ct * MAPS:(ct + 1) * MAPS], scalar=ln2[:, ct, 5:6], in1=base_rows[:], op0=ALU.mult,
                        op1=ALU.add)
            bank.release([v])
            xq["ln2_free"] = [v, lns[-1]]
            xq["lg", b] = v
            xq["spilled", b] = [spilled, d, m]

        sk = {"free": []}

        def sinkhorn(batches):
            T = len(batches) * CT
            at = batches[0] * CT
            tiles = slice(logits_of(batches[0]), logits_of(batches[0]) + T)
            lgs = [xq["lg", b] for b in batches]
            skz, skp, skw, sku, skv, ska, skb, skr, pre, post, soft = (
                a[:, 0:T] for a in (skz_all, skp_all, skw_all, sku_all, skv_all, ska_all, skb_all, skr_all,
                                    pre_all, post_all, soft_all))

            def over_j(v):
                return v[:].unsqueeze(2).broadcast_to([P, T, STREAMS, STREAMS])

            def over_i(v):
                return v[:].unsqueeze(3).broadcast_to([P, T, STREAMS, STREAMS])

            def by_column(m):
                return m[:].rearrange("p t i j -> p t j i")

            def D(after, method, *args, **kwargs):
                return dve(after, s_skd, method, *args, **kwargs)

            def A(after, method, *args, **kwargs):
                return act(after, s_ska, method, *args, **kwargs)

            t = D([*lgs, *sk["free"]],
                  nc.vector.tensor_scalar, skz[:].rearrange("p t i j -> p t (i j)"), lg[:, tiles, 0:RES],
                  1.0 / SINKHORN_TAU, None, ALU.mult)
            yield

            def negative_lse(target, m, spread, t, first):
                t = D([t], nc.vector.tensor_reduce, skr[:], m, AX_X, ALU.max)
                yield
                t = D([t], nc.vector.tensor_tensor, skp[:], skw[:] if not first else skz[:], spread(skr),
                    ALU.subtract)
                yield
                t = A([t], nc.scalar.activation, skp[:], skp[:], ACT.Exp)
                yield
                t = D([t], nc.vector.tensor_reduce, ska[:], skp[:] if spread is over_i else by_column(skp), AX_X,
                    ALU.add)
                yield
                t = A([t], nc.scalar.activation, ska[:], ska[:], ACT.Ln)
                yield
                return D([t],
                         nc.vector.scalar_tensor_tensor, out=target[:], in0=ska[:], scalar=-1.0, in1=skr[:],
                         op0=ALU.mult, op1=ALU.subtract)

            t = yield from negative_lse(sku, skz[:], over_i, t, True)
            yield
            t = D([t], nc.vector.tensor_tensor, skw[:], skz[:], over_i(sku), ALU.add)
            yield
            t = yield from negative_lse(skv, by_column(skw), over_j, t, False)
            yield
            done = 1
            while True:
                t = D([t], nc.vector.tensor_tensor, skw[:], skz[:], over_i(sku), ALU.add)
                yield
                t = D([t], nc.vector.tensor_tensor, skw[:], skw[:], over_j(skv), ALU.add)
                yield
                t = A([t], nc.scalar.activation, skp[:], skw[:], ACT.Exp)
                yield
                if done == SINKHORN_ITERS:
                    break
                rounds = min(REFRESH, SINKHORN_ITERS - done)
                for r in range(rounds):
                    if r:
                        t = D([t], nc.vector.tensor_tensor, skw[:], skp[:], over_j(skb), ALU.mult)
                        yield
                    m = skw if r else skp
                    t = D([t], nc.vector.tensor_reduce, skr[:], m[:], AX_X, ALU.add)
                    yield
                    t = D([t], nc.vector.reciprocal, ska[:], skr[:])
                    yield
                    t = D([t], nc.vector.tensor_tensor, skw[:], skp[:], over_i(ska), ALU.mult)
                    yield
                    t = D([t], nc.vector.tensor_reduce, skr[:], by_column(skw), AX_X, ALU.add)
                    yield
                    t = D([t], nc.vector.reciprocal, skb[:], skr[:])
                    yield
                done += rounds
                for scaling, potential in ((ska, sku), (skb, skv)):
                    t = A([t], nc.scalar.activation, skr[:], scaling[:], ACT.Ln)
                    yield
                    t = D([t], nc.vector.tensor_tensor, potential[:], potential[:], skr[:], ALU.add)
                    yield
            t = D([t, c_gate], nc.vector.tensor_scalar, skp[:], skp[:], gates[:, 2:3], None, ALU.mult)
            yield
            diagonal = skp[:].rearrange("p t i j -> p t (i j)")[:, :, 0:RES:STREAMS + 1]
            t = D([t, *[tok for b in batches for tok in xq["spilled", b][1:]]],
                  nc.vector.scalar_tensor_tensor, out=diagonal, in0=diagonal, scalar=gates[:, 3:4], in1=sd_all[:,
                  at:at + T].unsqueeze(2).broadcast_to([P, T, STREAMS]), op0=ALU.add, op1=ALU.add)
            yield
            for k, target in enumerate((pre, post)):
                cols = slice(RES + k * STREAMS, RES + (k + 1) * STREAMS)
                wide = [P, T, STREAMS]
                t = D([t], nc.vector.tensor_reduce, soft[:, :, 0], lg[:, tiles, cols], AX_X, ALU.max)
                yield
                t = D([t],
                      nc.vector.tensor_tensor, target[:], lg[:, tiles, cols], soft[:, :,
                      0].unsqueeze(2).broadcast_to(wide), ALU.subtract)
                yield
                t = A([t], nc.scalar.activation, target[:], target[:], ACT.Exp)
                yield
                t = D([t], nc.vector.tensor_reduce, soft[:, :, 0], target[:], AX_X, ALU.add)
                yield
                t = D([t], nc.vector.reciprocal, soft[:, :, 1], soft[:, :, 0])
                yield
                t = D([t],
                      nc.vector.tensor_tensor, target[:], target[:], soft[:, :,
                      1].unsqueeze(2).broadcast_to(wide), ALU.mult)
                yield
            sk["done"] = t
            yield

        def mix(batches):
            skp, pre, post = skp_all, pre_all, post_all
            buffers, loaded = mix_ln, []
            last = batches[-1] == NB - 1
            if last:
                for ct in range(CT):
                    buffers.slots.append(Slot(ap=x_sb[:, ct, :], sem=s_mixld[1 + ct]))
                    buffers.slots[-1].free = list(x_free)

            def load_tile(tile):
                b, ct = batches[tile // CT], tile % CT
                slot = buffers.take()
                return slot, sp((xq["spilled", b][0], *slot.free), slot.sem,
                                nc.sync.dma_start, slot.ap, ln_spill[b, ct * P:(ct + 1) * P, :])

            for tile in range(len(batches) * CT):
                b, ct = batches[tile // CT], tile % CT
                tok = batches[0] * CT + tile
                slot_ln, t = loaded.pop(0) if loaded else load_tile(tile)
                ln = slot_ln.ap
                if tile + 1 < len(batches) * CT and buffers.ready():
                    loaded.append(load_tile(tile + 1))
                stream = [ln[:, j * COLS:(j + 1) * COLS] for j in range(STREAMS)]
                yield from pause(10)
                buf = mix_out.take()
                u = act((t, sk["done"], *buf.free), s_xpa,
                        nc.scalar.activation, buf.ap[:], stream[0], ACT.Copy, scale=pre[:, tile, 0:1])
                for j in range(1, STREAMS):
                    yield
                    u = dve((u,), s_xp,
                            nc.vector.scalar_tensor_tensor, out=buf.ap[:], in0=stream[j], scalar=pre[:, tile,
                            j:j + 1], in1=buf.ap[:], op0=ALU.mult, op1=ALU.add)
                yield
                def start(i):
                    o = mix_out.take()
                    return o, act((t, *o.free, sk["done"]), s_ma,
                                  nc.scalar.activation, o.ap[:], stream[0], ACT.Identity, bias=mean_all[:,
                                  tok:tok + 1], scale=skp[:, tile, i, 0:1])

                def add(i, j, o, v):
                    return dve((v,), s_md, nc.vector.scalar_tensor_tensor, out=o.ap[:], in0=stream[j],
                        scalar=skp[:, tile, i, j:j + 1],
                               in1=o.ap[:], op0=ALU.mult, op1=ALU.add)

                o, v = start(0)
                yield from pause(2)
                while not split_bg.ready():
                    yield
                slot = split_bg.take()
                bank, u = transposed([buf.ap[:, j * P:(j + 1) * P] for j in range(KT)], (u,))
                buf.release([u])
                v = add(0, 1, o, v)
                yield from pause(2)
                th = split_high(bank, u, slot, BANK)
                v = add(0, 2, o, v)
                yield from pause(1)
                tokens = th, split_low(bank, th, slot, BANK)
                yield from pause(2)
                bank = tbank.take()
                for k in range(KT):
                    y = products(bank.ap[:, 0:COLS], [slot.h[:, k * P:(k + 1) * P], slot.l[:, k * P:(k + 1) * P]],
                                 [w[:, k, :] for w in wb], (*bank.free, *tokens, *w_ready["b"]), s_y, k == 0,
                                 k == KT - 1)
                v = add(0, 3, o, v)
                following = start(1)
                yield from pause(1)
                if last:
                    w = add(1, 1, *following)
                    w = add(1, 2, following[0], w)
                    following = following[0], add(1, 3, following[0], w)
                yield from pause(1)
                y = act((y, *y_sb.free), s_ya, nc.scalar.copy, y_sb.ap[:], bank.ap[:, 0:COLS])
                slot.release([y])
                bank.release([y])
                yield
                for i in range(STREAMS):
                    if i:
                        o, v = following or start(i)
                        if not (last and i == 1):
                            yield
                            for j in range(1, STREAMS):
                                v = add(i, j, o, v)
                                yield
                        following = None
                    v = dve((v, y), s_md,
                            nc.vector.scalar_tensor_tensor, out=o.ap[:], in0=y_sb.ap[:], scalar=post[:, tile,
                            i:i + 1], in1=o.ap[:], op0=ALU.mult, op1=ALU.add)
                    w = sp((v,), o.sem, nc.sync.dma_start, out[b, ct * P:(ct + 1) * P, i * COLS:(i + 1) * COLS],
                        o.ap[:])
                    o.release([w])
                    yield
                y_sb.release([v])
                slot_ln.release([v])
                yield
            sk["free"] = [v]

        def after_batch(b):
            yield from normalise_rows(b)
            if b + 1 < NB:
                yield from query_prepare(b + 1)

        def group_work(batches):
            yield from sinkhorn(batches)
            yield from mix(batches)

        nc.scalar.preload_act_table_set("natural_log_exp_and_others")
        for _ in (*load_context(0), *query_prepare(0)):
            pass
        TICKS = 220
        CHAIN, TILE, PAUSES = 370, 31, 26
        ends, at = {}, 0
        for size in GROUPS:
            at += size
            ends[at - 1] = list(range(at - size, at))
        written = []
        for b in range(NB):
            chain = keys(b, written)
            if b + 1 < NB:
                urgent.append(load_context(b + 1))
            written = queries(b, chain, b + 1 < NB)
            finish(urgent)
            urgent.append(after_batch(b))
            if b in ends:
                finish(steady)
                finish(urgent)
                steady.append(group_work(ends[b]))
                following = [n for n in ends if n > b]
                if following:
                    n = len(ends[b])
                    pace[0] = (CHAIN + TILE * n * CT) / (TICKS * (following[0] - b) - PAUSES * n * CT)
        finish(urgent)
        finish(steady)
        for s in (*s_out, s_spill):
            sp.wait(s, s.value)

        block = stack.enter_context(nc.Block())

        @block.sync
        def _(e):
            sp.replay()

        @block.tensor
        def _(e):
            pe.replay()

        @block.vector
        def _(e):
            dve.replay()

        @block.scalar
        def _(e):
            act.replay()

        @block.gpsimd
        def _(e):
            pool.replay()


def kernel(x, ctx_4096, L0_xattn_Wq, L0_xattn_Wk, L0_xattn_Wv, L0_xattn_Wo, L0_xattn_bo, L0_xattn_g, L0_ffn_W_res,
           L0_ffn_W_pre, L0_ffn_W_post, L0_ffn_H_res_base, L0_ffn_H_pre_base, L0_ffn_H_post_base, L0_ffn_gate,
           L0_ffn_W_branch):
    import numpy as np
    import concourse.bacc as bacc
    from concourse.bass_utils import run_bass_kernel_spmd

    host = {
        "x": x,
        "ctx": ctx_4096,
        "ctx_t": np.swapaxes(ctx_4096, 1, 2),
        "wq_t": np.transpose(L0_xattn_Wq),
        "wk_t": np.transpose(L0_xattn_Wk),
        "wv_t": np.transpose(L0_xattn_Wv),
        "wo_t": np.transpose(L0_xattn_Wo),
        "bo": L0_xattn_bo,
        "g": np.transpose(np.reshape(L0_xattn_g, (-1, P))),
        "w_maps_t": np.transpose(np.concatenate([L0_ffn_W_res, L0_ffn_W_pre, L0_ffn_W_post], axis=0)),
        "base": np.concatenate([np.reshape(L0_ffn_H_res_base, (-1,)), L0_ffn_H_pre_base, L0_ffn_H_post_base]),
        "gate": L0_ffn_gate,
        "w_branch": L0_ffn_W_branch,
    }
    nc = bacc.Bacc("TRN2", target_bir_lowering=False, num_devices=1)
    arrays, aps = {}, []
    for name, a in host.items():
        a = np.ascontiguousarray(a)
        arrays[f"in_{name}"] = a
        aps.append(nc.dram_tensor(f"in_{name}", a.shape, mybir.dt.from_np(a.dtype), kind="ExternalInput").ap())
    shape = tuple(x.shape)
    aps.append(nc.dram_tensor("ln_spill", shape, F32, kind="Internal").ap())
    aps.append(nc.dram_tensor("out_0", shape, F32, kind="ExternalOutput").ap())
    xattn_ffn(nc, *aps)
    r = run_bass_kernel_spmd(nc, [arrays], core_ids=[0])
    return r.results[0]["out_0"]
```
